# Optimizing a Trainium2 kernel written in Bass

```python
import numpy as np
import jax
import jax.numpy as jnp

def _softmax(x, axis=-1):
    return jax.nn.softmax(x, axis=axis)

def _gelu(x):
    return jax.nn.gelu(x, approximate=True)

def _silu(x):
    return jax.nn.silu(x)

def _sigmoid(x):
    return jax.nn.sigmoid(x)

def _layernorm(x, axis=-1, eps=1e-05):
    m = jnp.mean(x, axis=axis, keepdims=True)
    v = jnp.var(x, axis=axis, keepdims=True)
    return (x - m) / jnp.sqrt(v + eps)

def _scatter_add(tgt, idx, src, axis=0):
    return tgt.at[idx].add(src)

def _segment_sum(src, seg, n):
    return jax.ops.segment_sum(src, seg, n)
kernel_name = 'mk_xattn_ffn_d1_seqx_r4_89a1b2'

def setup_inputs(seed: int=0):
    np.random.seed(seed)
    _w = jnp.asarray

    def _rec_inputs():
        import jax
        import jax.numpy as jnp
        _rk = jax.random.key(seed)
        x = -0.0005207 + 1.001 * jax.random.normal(jax.random.fold_in(_rk, 1), (4, 1024, 256), jnp.float32)
        _lenS = 1024 - jax.random.randint(jax.random.fold_in(_rk, 7), (4,), 0, max(1, 1024 // 4) + 1, jnp.int32)
        _lenS2 = 154 - jax.random.randint(jax.random.fold_in(_rk, 8), (4,), 0, max(1, 154 // 4) + 1, jnp.int32)
        _ctx_1024P = jax.random.normal(jax.random.fold_in(_rk, 11), (4, 16, 256), jnp.float32)
        _ctx_1024c = jax.random.dirichlet(jax.random.fold_in(_rk, 511), 0.3 * jnp.ones((16,), jnp.float32), (4, 154))
        _ctx_1024t = jnp.einsum('bsk,bkd->bsd', _ctx_1024c, _ctx_1024P)
        _ctx_1024t = _ctx_1024t * jax.lax.rsqrt(jnp.mean(jnp.square(_ctx_1024t)) + 1e-12) * 0.953939
        ctx_1024 = -1.39393e-06 + 0.999914 * (_ctx_1024t + 0.3 * jax.random.normal(jax.random.fold_in(_rk, 611), (4, 154, 256), jnp.float32))
        itok_BxSx64_0_2047 = jax.random.randint(jax.random.fold_in(_rk, 12), (4, 1024, 64), 0, 512, jnp.int32)
        return (x, ctx_1024, itok_BxSx64_0_2047)
    x, ctx_1024, itok_BxSx64_0_2047 = _rec_inputs()

    def _L0_xattn_setup():
        import jax, jax.numpy as jnp
        import numpy as np
        B, NQ, NKV, K = (2, 256, 512, 64)
        D, H, LAT = (256, 16, 128)
        HD = D // H
        SCALE = 1.0 / np.sqrt(HD)
        key = jax.random.key(seed)
        ks = jax.random.split(key, 7)
        s = lambda fan_in: 1.0 / np.sqrt(fan_in)
        return {'x_q': jax.random.normal(ks[0], (B, NQ, D), jnp.float32), 'x_kv': jax.random.normal(ks[1], (B, NKV, D), jnp.float32), 'indices': jax.random.randint(ks[2], (B, NQ, K), 0, NKV), 'W_q': jax.random.normal(ks[3], (D, D), jnp.float32) * s(D), 'W_kv_down': jax.random.normal(ks[4], (LAT, D), jnp.float32) * s(D), 'W_kv_up': jax.random.normal(ks[5], (2 * D, LAT), jnp.float32) * s(LAT), 'W_out': jax.random.normal(ks[6], (D, D), jnp.float32) * s(D)}
    _L0_xattn_all = _L0_xattn_setup()
    _L0_xattn_in = {k: v for k, v in _L0_xattn_all.items() if k in ('W_q', 'W_kv_down', 'W_kv_up', 'W_out')}
    del _L0_xattn_all

    def _L0_ffn_setup():
        import jax, jax.numpy as jnp
        import numpy as np
        from jax import lax
        H, DK, DV, N_EXP, CHUNK = (8, 64, 64, 4, 64)
        LORA, GATE_LR = (64, 16)
        NORMALIZER = 16.0
        EPS = 1e-05

        def chunk_gla(q, k, v, gk, C=CHUNK):
            L, h, dk = q.shape
            dv = v.shape[-1]
            nc = L // C
            qc, kc, vc, gc = (t.reshape(nc, C, h, -1) for t in (q, k, v, gk))
            g = jnp.cumsum(gc, axis=1)
            g_last = g[:, -1]
            qg = qc * jnp.exp(g)
            kg = kc * jnp.exp(-g)
            A = jnp.einsum('cthd,cshd->chts', qg, kg)
            A = A * jnp.tril(jnp.ones((C, C), q.dtype))
            o_intra = jnp.einsum('chts,cshe->cthe', A, vc)
            k_out = kc * jnp.exp(g_last[:, None] - g)
            chunk_kv = jnp.einsum('cthd,cthe->chde', k_out, vc)
            decay = jnp.exp(g_last)

            def step(S, inp):
                kv, dec, qg_c = inp
                o_inter = jnp.einsum('thd,hde->the', qg_c, S)
                return (S * dec[..., None] + kv, o_inter)
            S0 = jnp.zeros((h, dk, dv), q.dtype)
            _, o_inter = lax.scan(step, S0, (chunk_kv, decay, qg))
            return (o_intra + o_inter).reshape(L, h, dv)
        key = jax.random.key(seed)
        ks = jax.random.split(key, 20)
        B, L, Dh = (1, 1024, 256)
        KD, VD = (H * DK, H * DV)
        w = lambda i, shape: jax.random.normal(ks[i], shape, jnp.float32) * 0.02
        return {'x': jax.random.normal(ks[0], (B, L, Dh), jnp.float32), 'Wq': w(1, (Dh, KD)), 'Wk': w(2, (Dh, KD)), 'Wv': w(3, (Dh, VD)), 'Wqa': w(4, (Dh, LORA)), 'Wqb': w(5, (LORA, KD)), 'Wka': w(6, (Dh, LORA)), 'Wkb': w(7, (LORA, KD)), 'Wg1a': w(8, (Dh, GATE_LR)), 'Wg1b': w(9, (GATE_LR, KD)), 'bg1': jnp.zeros((KD,), jnp.float32), 'Wg2a': w(10, (Dh, GATE_LR)), 'Wg2b': w(11, (GATE_LR, KD)), 'bg2': jnp.zeros((KD,), jnp.float32), 'We': w(12, (Dh, N_EXP)), 'Wga': w(13, (Dh, LORA)), 'Wgb': w(14, (LORA, VD)), 'norm_w': jnp.ones((DV,), jnp.float32), 'Wo': w(15, (VD, Dh))}
    _L0_ffn_all = _L0_ffn_setup()
    _L0_ffn_in = {k: v for k, v in _L0_ffn_all.items() if k in ('Wq', 'Wk', 'Wv', 'Wqa', 'Wqb', 'Wka', 'Wkb', 'Wg1a', 'Wg1b', 'bg1', 'Wg2a', 'Wg2b', 'bg2', 'We', 'Wga', 'Wgb', 'norm_w', 'Wo')}
    del _L0_ffn_all
    return {'x': x, 'ctx_1024': ctx_1024, 'itok_BxSx64_0_2047': itok_BxSx64_0_2047, 'L0_xattn_W_q': _L0_xattn_in['W_q'], 'L0_xattn_W_kv_down': _L0_xattn_in['W_kv_down'], 'L0_xattn_W_kv_up': _L0_xattn_in['W_kv_up'], 'L0_xattn_W_out': _L0_xattn_in['W_out'], 'L0_ffn_Wq': _L0_ffn_in['Wq'], 'L0_ffn_Wk': _L0_ffn_in['Wk'], 'L0_ffn_Wv': _L0_ffn_in['Wv'], 'L0_ffn_Wqa': _L0_ffn_in['Wqa'], 'L0_ffn_Wqb': _L0_ffn_in['Wqb'], 'L0_ffn_Wka': _L0_ffn_in['Wka'], 'L0_ffn_Wkb': _L0_ffn_in['Wkb'], 'L0_ffn_Wg1a': _L0_ffn_in['Wg1a'], 'L0_ffn_Wg1b': _L0_ffn_in['Wg1b'], 'L0_ffn_bg1': _L0_ffn_in['bg1'], 'L0_ffn_Wg2a': _L0_ffn_in['Wg2a'], 'L0_ffn_Wg2b': _L0_ffn_in['Wg2b'], 'L0_ffn_bg2': _L0_ffn_in['bg2'], 'L0_ffn_We': _L0_ffn_in['We'], 'L0_ffn_Wga': _L0_ffn_in['Wga'], 'L0_ffn_Wgb': _L0_ffn_in['Wgb'], 'L0_ffn_norm_w': _L0_ffn_in['norm_w'], 'L0_ffn_Wo': _L0_ffn_in['Wo']}

def reference(x, ctx_1024, itok_BxSx64_0_2047, L0_xattn_W_q, L0_xattn_W_kv_down, L0_xattn_W_kv_up, L0_xattn_W_out, L0_ffn_Wq, L0_ffn_Wk, L0_ffn_Wv, L0_ffn_Wqa, L0_ffn_Wqb, L0_ffn_Wka, L0_ffn_Wkb, L0_ffn_Wg1a, L0_ffn_Wg1b, L0_ffn_bg1, L0_ffn_Wg2a, L0_ffn_Wg2b, L0_ffn_bg2, L0_ffn_We, L0_ffn_Wga, L0_ffn_Wgb, L0_ffn_norm_w, L0_ffn_Wo):
    import jax
    import jax.numpy as jnp

    def _L0_xattn_ref(x_q, x_kv, indices, W_q, W_kv_down, W_kv_up, W_out):
        import jax, jax.numpy as jnp
        import numpy as np
        B, NQ, NKV, K = (2, 256, 512, 64)
        D, H, LAT = (256, 16, 128)
        HD = D // H
        SCALE = 1.0 / np.sqrt(HD)
        b, nq, d = x_q.shape
        q = (x_q @ W_q.T).reshape(b, nq, H, HD)
        c_kv = x_kv @ W_kv_down.T
        c_sel = c_kv[jnp.arange(b)[:, None, None], indices]
        kv = (c_sel @ W_kv_up.T).reshape(b, nq, K, 2, H, HD)
        k = kv[:, :, :, 0]
        v = kv[:, :, :, 1]
        scores = jnp.einsum('bqhd,bqkhd->bqkh', q, k) * SCALE
        attn = jax.nn.softmax(scores, axis=2)
        out = jnp.einsum('bqkh,bqkhd->bqhd', attn, v).reshape(b, nq, d)
        return out @ W_out.T

    def _L0_ffn_ref(x, Wq, Wk, Wv, Wqa, Wqb, Wka, Wkb, Wg1a, Wg1b, bg1, Wg2a, Wg2b, bg2, We, Wga, Wgb, norm_w, Wo):
        import jax, jax.numpy as jnp
        import numpy as np
        from jax import lax
        H, DK, DV, N_EXP, CHUNK = (8, 64, 64, 4, 64)
        LORA, GATE_LR = (64, 16)
        NORMALIZER = 16.0
        EPS = 1e-05

        def chunk_gla(q, k, v, gk, C=CHUNK):
            L, h, dk = q.shape
            dv = v.shape[-1]
            nc = L // C
            qc, kc, vc, gc = (t.reshape(nc, C, h, -1) for t in (q, k, v, gk))
            g = jnp.cumsum(gc, axis=1)
            g_last = g[:, -1]
            qg = qc * jnp.exp(g)
            kg = kc * jnp.exp(-g)
            A = jnp.einsum('cthd,cshd->chts', qg, kg)
            A = A * jnp.tril(jnp.ones((C, C), q.dtype))
            o_intra = jnp.einsum('chts,cshe->cthe', A, vc)
            k_out = kc * jnp.exp(g_last[:, None] - g)
            chunk_kv = jnp.einsum('cthd,cthe->chde', k_out, vc)
            decay = jnp.exp(g_last)

            def step(S, inp):
                kv, dec, qg_c = inp
                o_inter = jnp.einsum('thd,hde->the', qg_c, S)
                return (S * dec[..., None] + kv, o_inter)
            S0 = jnp.zeros((h, dk, dv), q.dtype)
            _, o_inter = lax.scan(step, S0, (chunk_kv, decay, qg))
            return (o_intra + o_inter).reshape(L, h, dv)
        B, L, Dh = x.shape
        scale = DK ** (-0.5)
        q1 = (x @ Wq).reshape(B, L, H, DK) * scale
        k1 = (x @ Wk).reshape(B, L, H, DK)
        v = (x @ Wv).reshape(B, L, H, DV)
        q2 = (x @ Wqa @ Wqb).reshape(B, L, H, DK) * scale
        k2 = jax.nn.softmax((x @ Wka @ Wkb).reshape(B, L, H, DK), axis=-1)
        gk1 = (jax.nn.log_sigmoid(x @ Wg1a @ Wg1b + bg1) / NORMALIZER).reshape(B, L, H, DK)
        gk2 = (jax.nn.log_sigmoid(x @ Wg2a @ Wg2b + bg2) / NORMALIZER).reshape(B, L, H, DK)
        e = jax.nn.softmax(x @ We, axis=-1)
        _, idx = lax.top_k(e, 1)
        mask = jax.nn.one_hot(idx, N_EXP, dtype=x.dtype).sum(-2)
        rw = e * mask
        fac = jnp.swapaxes(rw, 1, 2)[:, :, :, None, None]
        mfac = jnp.swapaxes(mask, 1, 2)[:, :, :, None, None]
        q_e = q2[:, None] * fac
        k_e = k2[:, None] * fac
        gk_e = gk2[:, None] * mfac
        gla_b = jax.vmap(chunk_gla)
        o_dense = gla_b(q1, k1, v, gk1)
        gla_be = jax.vmap(jax.vmap(chunk_gla, in_axes=(0, 0, None, 0)))
        o_sparse = gla_be(q_e, k_e, v, gk_e).sum(axis=1)
        o = o_dense + o_sparse
        g = (x @ Wga @ Wgb).reshape(B, L, H, DV)
        o = o * lax.rsqrt(jnp.mean(o * o, axis=-1, keepdims=True) + EPS) * norm_w
        o = o * (g * jax.nn.sigmoid(g))
        return o.reshape(B, L, H * DV) @ Wo
    x = x + _L0_xattn_ref(_layernorm(x, axis=-1), ctx_1024, itok_BxSx64_0_2047, L0_xattn_W_q, L0_xattn_W_kv_down, L0_xattn_W_kv_up, L0_xattn_W_out)
    x = x + _L0_ffn_ref(_layernorm(x, axis=-1), L0_ffn_Wq, L0_ffn_Wk, L0_ffn_Wv, L0_ffn_Wqa, L0_ffn_Wqb, L0_ffn_Wka, L0_ffn_Wkb, L0_ffn_Wg1a, L0_ffn_Wg1b, L0_ffn_bg1, L0_ffn_Wg2a, L0_ffn_Wg2b, L0_ffn_bg2, L0_ffn_We, L0_ffn_Wga, L0_ffn_Wgb, L0_ffn_norm_w, L0_ffn_Wo)
    return x

_drawn_inputs = setup_inputs


def setup_inputs(seed=0):
    import zlib

    import numpy as np

    out = dict(_drawn_inputs(seed))
    spreads = {'L0_ffn_bg1': (0.0, 0.8), 'L0_ffn_bg2': (0.0, 2.0), 'L0_ffn_norm_w': (1.0, 0.6)}
    factors = {'L0_ffn_Wq': 5.822,
     'L0_ffn_Wk': 6.1,
     'L0_ffn_Wv': 5.995,
     'L0_ffn_Wqa': 8.0,
     'L0_ffn_Wqb': 8.0,
     'L0_ffn_Wka': 8.0,
     'L0_ffn_Wkb': 8.0,
     'L0_ffn_Wg1a': 8.0,
     'L0_ffn_Wg1b': 8.0,
     'L0_ffn_Wg2a': 8.0,
     'L0_ffn_Wg2b': 8.0,
     'L0_ffn_We': 8.0,
     'L0_ffn_Wga': 6.011,
     'L0_ffn_Wgb': 5.921,
     'L0_ffn_Wo': 5.988}
    for name, (base, spread) in spreads.items():
        noise = np.random.default_rng([zlib.crc32(name.encode()), seed]).standard_normal(out[name].shape)
        drawn = base * np.exp(spread * noise) if base else spread * noise
        out[name] = jnp.asarray(drawn.astype(out[name].dtype))
    for name, factor in factors.items():
        out[name] = (out[name] * factor).astype(out[name].dtype)
    return out
```

```python
import numpy as np
import concourse.bass as bass
from concourse import mybir
from contextlib import ExitStack

P = 128
B, L, D = 4, 1024, 256
TILES = B * L // P
TPB = L // P
KD = D // P
NKV, PICKS = 154, 64
HA, DA = 16, 16
REST = NKV - P
RPAD, NPAD = 32, 160
BASES, DIGIT = 52, 7
GROUPS, GH = 4, 4
VW = DA + 1
H, DK = 8, 64
HD = H * DK
NP = HD // P
NE = 4
ST = NE + 1
NORMALIZER = 16.0
EPS = 1e-5
MASKED = -1e30

_C = {}
_n = 0
for _name, _w in (("ident", P), ("cum", P), ("tri", P), ("half", 2), ("prio", NE), ("onerow", 1), ("eps", 1),
                  ("bases", BASES), ("even_odd", 2), ("quarter", GH), ("keep", TILES)):
    _C[_name] = (_n, _n + _w)
    _n += _w
NCONST = _n


def constants():
    c = np.zeros((P, NCONST), np.float32)
    r = np.arange(P)
    s, t = r[:, None], r[None, :]
    mid = P // 2

    def put(name, v):
        c[:, _C[name][0]:_C[name][1]] = v

    put("ident", s == t)
    put("cum", (((s >= mid) & (s <= t)) * 1.0 - ((s < mid) & (s > t)) * 1.0) / NORMALIZER)
    put("tri", s <= t)
    put("half", np.stack([r < mid, r >= mid], 1) / NORMALIZER)
    put("prio", np.arange(NE, 0, -1)[None, :])
    put("onerow", ((r == 80) | (r == 112))[:, None])
    put("eps", EPS)
    put("bases", np.arange(BASES)[None, :])
    put("even_odd", np.stack([(r // DA) % 2 == 0, (r // DA) % 2 == 1], 1) * DA ** -0.5)
    put("quarter", (r // RPAD)[:, None] == np.arange(GH)[None, :])
    put("keep", (np.arange(TILES) % TPB != 0)[None, :])
    return c


class Steps:

    def __init__(self, nc, ctx):
        self.nc, self.ctx = nc, ctx
        self.engines = {"pe": nc.tensor, "dve": nc.vector, "act": nc.scalar, "pool": nc.gpsimd, "sp": nc.sync}
        self.gate = ctx.enter_context(nc.semaphore("gate"))
        self.sems, self.total, self.number = {}, {}, {}
        self.dry = True
        self.tile = {}
        self.waited = {}

    def begin(self, half, tile):
        self.tile[half] = tile
        for key in [k for k in self.waited if k[0] == half]:
            del self.waited[key]

    def do(self, half, engine, name, after, issue, dma=False, apart=False):
        lane = (half, name if dma else engine)
        if self.dry:
            self.total[lane] = self.total.get(lane, 0) + 1
            if lane not in self.sems:
                self.sems[lane] = self.ctx.enter_context(self.nc.semaphore("done_" + "_".join(lane)))
            self.number[f"{half}.{name}"] = (lane, self.total[lane], 16 if dma else 1)
            return
        for a in after:
            self.wait(half, engine, a)
        if apart and after:
            self.engines[engine].sem_inc(self.gate, 1)
        issue().then_inc(self.sems[lane], 16 if dma else 1)

    def wait(self, half, engine, what):
        before = what.startswith("<")
        name = what.lstrip("<")
        if "." not in name:
            name = f"{half}.{name}"
        lane, number, unit = self.number[name]
        tile = self.tile[half]
        if before and isinstance(tile, int) and tile == 0:
            return
        seen = self.waited.get((half, engine, lane), (-1, 0))
        if (0 if before else 1, number) <= seen:
            return
        self.waited[(half, engine, lane)] = (0 if before else 1, number)
        value = (tile * self.total[lane] + (number - self.total[lane] * before)) * unit
        self.engines[engine].wait_ge(self.sems[lane], value)


def program(nc, x, idx, ctxT, consts, w_q, w_down, w_up, w_out, wa, we, wq, wk, wv, wqk_b, wg_b, wo, norm_w, out):
    f32, bf16, i32 = mybir.dt.float32, mybir.dt.bfloat16, mybir.dt.int32
    ALU, ACT, AX = mybir.AluOpType, mybir.ActivationFunctionType, mybir.AxisListType
    pe, dve, act, pool, sp = nc.tensor, nc.vector, nc.scalar, nc.gpsimd, nc.sync

    with ExitStack() as ctx:
        def sb(name, shape, dt=f32):
            return ctx.enter_context(nc.sbuf_tensor(name, shape, dt))

        def ps(name, shape):
            return ctx.enter_context(nc.psum_tensor(name, shape, f32))

        def sem(name):
            return ctx.enter_context(nc.semaphore(name))

        CONST = sb("CONST", [P, NCONST])

        def const(name):
            return CONST[:, _C[name][0]:_C[name][1]]

        ident, cum, tri = const("ident"), const("cum"), const("tri")
        prio, eps = const("prio"), const("eps")
        WQ_A = sb("WQ_A", [P, KD, D])
        WDOWN = sb("WDOWN", [P, KD, P])
        WUP = sb("WUP", [P, 2 * D])
        WOUT = sb("WOUT", [P, KD, D])
        CTXT = sb("CTXT", [P, KD, B * NKV])
        WA = sb("WA", [P, KD, 256])
        WE = sb("WE", [P, KD, NE])
        WQ = sb("WQ", [P, KD, HD])
        WK = sb("WK", [P, KD, HD])
        WV = sb("WV", [P, KD, HD])
        WQKB = sb("WQKB", [P, HD])
        WGB = sb("WGB", [P, HD])
        WO = sb("WO", [P, NP, D])
        NORMW = sb("NORMW", [P, 1])
        identb = sb("identb", [P, P], bf16)
        BASETAB = sb("BASETAB", [P, BASES, PICKS], bf16)
        CT = sb("CT", [P, B, NKV])
        CREST = sb("CREST", [P, B, GH, RPAD])
        KALL = sb("KALL", [P, KD, B, 2, NKV])
        VALL = sb("VALL", [P, B, HA, VW])
        VRALL = sb("VRALL", [P, B, GROUPS * GH * VW])
        KNOW = sb("KNOW", [P, KD, 2, NKV])
        VNOW = sb("VNOW", [P, HA, VW])
        VRNOW = sb("VRNOW", [P, GROUPS * GH * VW])

        XA = sb("XA", [P, D])
        XB = sb("XB", [P, D])
        IDX = sb("IDX", [P, PICKS], i32)
        IW = [sb(f"IW{i}", [P, PICKS]) for i in range(6)]
        BASE = sb("BASE", [P, PICKS], bf16)
        WEIGHT = sb("WEIGHT", [P, PICKS], bf16)
        HOT = sb("HOT", [P, BASES, PICKS], bf16)
        PACKED = sb("PACKED", [P, BASES], i32)
        COUNTI = sb("COUNTI", [P, NPAD], i32)
        COUNT = sb("COUNT", [P, NPAD])
        COUNTR = sb("COUNTR", [P, GH, RPAD])
        MASK = sb("MASK", [P, NKV], bf16)
        COUNTT = sb("COUNTT", [P, 2, P])
        STATS = sb("STATS", [P, 6])
        MV = sb("MV", [P, 2])
        RSTD = sb("RSTD", [P, 2])
        XN = sb("XN", [P, D])
        XNT = sb("XNT", [P, KD, P])
        QT = sb("QT", [P, KD, P])
        MAXS = sb("MAXS", [P, 2, GH])
        SHIFTED = sb("SHIFTED", [P, 2, GH * NPAD])
        EXPS = sb("EXPS", [P, 2, GH * NPAD])
        PT = sb("PT", [P, GH, P])
        PR = sb("PR", [P, P])
        RSUM = sb("RSUM", [P, HA])
        ON = sb("ON", [P, D])
        ONT = sb("ONT", [P, KD, P])
        X1 = sb("X1", [P, D])

        X1B = sb("X1B", [P, D])
        STATS2 = sb("STATS2", [P, 6])
        MV2 = sb("MV2", [P, 2])
        RSTD2 = sb("RSTD2", [P, 2])
        XM = sb("XM", [P, D])
        XMT = sb("XMT", [P, KD, P])
        HID1 = sb("HID1", [P, P])
        HID2 = sb("HID2", [P, P])
        HQ = sb("HQ", [P, P])
        LOGIT = sb("LOGIT", [P, NE])
        RT = sb("RT", [P, 8])
        VALS = sb("VALS", [P, NE])
        ELOG = sb("ELOG", [P, NE])
        ISEXP = sb("ISEXP", [P, NE])
        LABB = sb("LABB", [P, 1], bf16)
        HALFE = sb("HALFE", [P, 2, NE])
        CUME = sb("CUME", [P, P])
        TRIE = sb("TRIE", [P, P])
        ISEXPT = sb("ISEXPT", [P, NE, P])
        SP3 = sb("SP3", [P, 3, HD])
        LS3 = sb("LS3", [P, 3, HD])
        SG = sb("SG", [P, HD])
        V = sb("V", [P, HD])
        EP1 = sb("EP1", [P, HD])
        EN1 = sb("EN1", [P, HD])
        EP2 = sb("EP2", [P, HD])
        EN2 = sb("EN2", [P, HD])
        K2 = sb("K2", [P, H, DK])
        KS = sb("KS", [P, 4, H])
        KG1T = sb("KG1T", [P, NP, P])
        KG2T = sb("KG2T", [P, NP, P])
        QG2 = sb("QG2", [P, NP, P])
        QM = sb("QM", [P, ST, NP, P])
        KGM = sb("KGM", [P, ST, HD])
        AT1 = sb("AT1", [P, 2, NP, P])
        AT2 = sb("AT2", [P, 2, NP, P])
        EG = sb("EG", [P, 2, ST, NP])
        ELAST = sb("ELAST", [P, ST, NP])
        DEC = sb("DEC", [P, ST, NP])
        STATE = sb("STATE", [P, ST, NP, DK])
        SQ = sb("SQ", [P, H, DK])
        RMS = sb("RMS", [P, 2, H])
        OG = sb("OG", [P, H, DK])
        OGT = sb("OGT", [P, NP, P])
        OUT = sb("OUT", [P, D])

        SA = ps("SA", [P, 2, 512])
        TA = ps("TA", [P, 512])
        MA = ps("MA", [P, 512])
        F = ps("F", [P, 4, 512])

        s_w = sem("s_w")
        s_pe0 = sem("s_pe0")
        s_dve0 = sem("s_dve0")
        s_act0 = sem("s_act0")
        steps = Steps(nc, ctx)

        loads = [(CONST[:, :], consts), (CTXT[:, :, :], ctxT), (WDOWN[:, :, :], w_down), (WUP[:, :], w_up),
                 (WQ_A[:, :, :], w_q), (WOUT[:, :, :], w_out), (WA[:, :, :], wa), (WE[:, :, :], we),
                 (WQ[:, :, :], wq), (WK[:, :, :], wk), (WV[:, :, :], wv), (WQKB[:, :], wqk_b), (WGB[:, :], wg_b),
                 (WO[:, :, :], wo), (NORMW[:, :], norm_w)]
        for n, (dst, src) in enumerate(loads):
            (sp if n % 2 == 0 else act).dma_start(dst, src).then_inc(s_w, 16)
        act.preload_act_table_set("natural_log_exp_and_others")
        pool.memset(CREST[:, :, :, :], 0.0).then_inc(s_act0, 1)
        for e in (pe, dve, act, pool):
            e.wait_ge(s_w, 16 * len(loads))
        half = 2 * NKV
        for c in range(2):
            for k in range(KD):
                last = pe.matmul(F[:, c, 0:half], WDOWN[:, k, :], CTXT[:, k, c * half:(c + 1) * half],
                                 start=k == 0, stop=k == KD - 1)
        last.then_inc(s_pe0, 1)
        dve.wait_ge(s_pe0, 1)
        CTf = CT[:, :, :].rearrange("p b j -> p (b j)")
        for c in range(2):
            last = dve.tensor_copy(CTf[:, c * half:(c + 1) * half], F[:, c, 0:half])
        last.then_inc(s_dve0, 1)
        dve.wait_ge(s_dve0, 1)
        dve.wait_ge(s_act0, 1)
        for hh in range(GH):
            last = dve.tensor_copy(CREST[:, :, hh, 0:REST], CT[:, :, P:NKV])
        last.then_inc(s_dve0, 1)
        pe.wait_ge(s_dve0, 1)
        for blk in range(KD):
            for c in range(2):
                bank = SA[:, c, 0:half] if blk == 0 else (TA, MA)[c][:, 0:half]
                last = pe.matmul(bank, WUP[:, blk * P:(blk + 1) * P], CTf[:, c * half:(c + 1) * half],
                                 start=True, stop=True)
        last.then_inc(s_pe0, 1)
        dve.wait_ge(s_pe0, 2)
        for blk in range(KD):
            for c in range(2):
                bank = SA[:, c, 0:half] if blk == 0 else (TA, MA)[c][:, 0:half]
                for odd in range(2):
                    dve.tensor_scalar(KALL[:, blk, 2 * c:2 * c + 2, odd, :],
                                      bank.rearrange("p (b j) -> p b j", b=2),
                                      const("even_odd")[:, odd:odd + 1], None, ALU.mult)
        pe.wait_ge(s_dve0, 2)
        for b in range(B):
            pe.matmul(F[:, b, 0:D], CT[:, b, 0:P], WUP[:, D:2 * D], start=True, stop=True)
            last = pe.matmul(F[:, b, D:2 * D], CREST[:, b, :, :].rearrange("p h j -> p (h j)"), WUP[:, D:2 * D], start=True, stop=True)
        last.then_inc(s_pe0, 1)
        dve.wait_ge(s_pe0, 3)
        dve.memset(VALL[:, :, :, DA:VW], 1.0)
        VR5 = VRALL[:, :, :].rearrange("p b (g h w) -> p b g h w", g=GROUPS, h=GH)
        for b in range(B):
            dve.tensor_copy(VALL[:, b, :, 0:DA], F[:, b, 0:D].rearrange("p (h d) -> p h d", d=DA))
            rest = F[:, b, D:2 * D].rearrange("p (g h d) -> p g h d", g=GROUPS, h=GH)
            for hh in range(GH):
                quarter = const("quarter")[:, hh:hh + 1]
                dve.tensor_scalar(VR5[:, b, :, hh, 0:DA], rest[:, :, hh, :], quarter, None, ALU.mult)
                dve.tensor_copy(VR5[:, b, :, hh, DA:VW], quarter.unsqueeze(1).to_broadcast([P, GROUPS, 1]))
        for p in range(NP):
            dve.tensor_scalar(WO[:, p, :], WO[:, p, :], NORMW[:, 0:1], None, ALU.mult)
        dve.tensor_copy(identb[:, :], ident)
        dve.tensor_copy(BASETAB[:, :, :], const("bases").unsqueeze(2).to_broadcast([P, BASES, PICKS]))
        pool.memset(COUNTI[:, :], 0)
        pool.memset(SHIFTED[:, :, :], 0.0)
        pool.memset(STATE[:, :, :, :], 0.0)
        pool.memset(ELAST[:, :, :], 0.0)
        nc.all_engine_barrier()

        def att(t):
            steps.begin("att", t)

            def do(engine, name, after, issue, dma=False, apart=False):
                steps.do("att", engine, name, after, issue, dma, apart)

            rows = bass.ts(t, P)
            do("sp", "load_idx", ["<idx_float"], lambda: sp.dma_start(IDX[:, :], idx[rows, :]), dma=True)
            do("sp", "load_xa", ["<xn"], lambda: sp.dma_start(XA[:, :], x[rows, :]), dma=True)
            do("sp", "load_xb", ["<x1"], lambda: sp.dma_start(XB[:, :], x[rows, :]), dma=True)
            do("pool", "idx_float", ["load_idx", "<idx_clamp"], lambda: pool.tensor_copy(IW[1][:, :], IDX[:, :]), apart=True)
            do("pool", "idx_wrap1", ["idx_float"],
               lambda: pool.tensor_scalar(IW[0][:, :], IW[1][:, :], 0.0, float(NKV), ALU.is_lt, ALU.mult), apart=True)
            do("pool", "idx_wrap2", ["idx_wrap1"],
               lambda: pool.tensor_tensor(IW[1][:, :], IW[1][:, :], IW[0][:, :], ALU.add))
            do("pool", "idx_clamp", ["idx_wrap2", "<weight"],
               lambda: pool.tensor_scalar(IW[2][:, :], IW[1][:, :], float(NKV - 1), 0.0, ALU.min, ALU.max), apart=True)
            yield
            do("pool", "digit1", ["idx_clamp"],
               lambda: pool.tensor_scalar(IW[3][:, :], IW[2][:, :], float(BASES), None, ALU.is_ge), apart=True)
            do("pool", "digit2", [],
               lambda: pool.tensor_scalar(IW[4][:, :], IW[2][:, :], float(2 * BASES), None, ALU.is_ge))
            do("dve", "digits", ["digit2"],
               lambda: dve.tensor_tensor(IW[5][:, :], IW[3][:, :], IW[4][:, :], ALU.add))
            do("dve", "weight1", ["digits"],
               lambda: dve.tensor_scalar(IW[3][:, :], IW[3][:, :], float(2 ** DIGIT - 1), 1.0, ALU.mult, ALU.add))
            do("dve", "base", ["digits", "<hot"],
               lambda: dve.scalar_tensor_tensor(BASE[:, :], IW[5][:, :], float(-BASES), IW[2][:, :], ALU.mult, ALU.add))
            do("dve", "weight", ["weight1", "<hotw"],
               lambda: dve.scalar_tensor_tensor(WEIGHT[:, :], IW[4][:, :], float(4 ** DIGIT - 2 ** DIGIT), IW[3][:, :],
                                                ALU.mult, ALU.add))
            do("dve", "stats", ["load_xa"], lambda: dve.bn_stats(STATS[:, :], XA[:, :]))
            do("dve", "meanvar", ["stats"], lambda: dve.bn_aggr(MV[:, :], STATS[:, :]), apart=True)
            do("act", "lnvar", ["meanvar"], lambda: act.activation(RSTD[:, 0:1], MV[:, 1:2], ACT.Ln, bias=eps))
            do("act", "rstd", ["lnvar"], lambda: act.activation(RSTD[:, 1:2], RSTD[:, 0:1], ACT.Exp, scale=-0.5))
            yield
            do("pool", "know", ["<scores_3"], lambda: pool.tensor_copy(KNOW[:, :, :, :], KALL[:, :, t // TPB, :, :]), apart=True)
            do("pool", "vnow", ["<values_3"], lambda: pool.tensor_copy(VNOW[:, :, :], VALL[:, t // TPB, :, :]), apart=True)
            do("pool", "vrnow", [], lambda: pool.tensor_copy(VRNOW[:, :], VRALL[:, t // TPB, :]))
            do("dve", "hot", ["weight"],
               lambda: dve.tensor_tensor(HOT[:, :, :], BASE[:, :].unsqueeze(1).to_broadcast([P, BASES, PICKS]),
                                         BASETAB[:, :, :], ALU.is_equal))
            do("dve", "xn", ["rstd", "<xt"],
               lambda: dve.tensor_scalar(XN[:, :], XA[:, :], MV[:, 0:1], RSTD[:, 1:2], ALU.subtract, ALU.mult))

            def transposes(dst, src, n):
                for k in range(n):
                    last = pe.transpose(dst[:, k * P:(k + 1) * P], src[:, k * P:(k + 1) * P], ident)
                return last

            do("pe", "xt_ps", ["xn", "<rsum", "<on"], lambda: transposes(MA[:, :], XN[:, :], KD))
            do("act", "xt", ["xt_ps"], lambda: act.activation(XNT[:, :, :].rearrange("p k t -> p (k t)"), MA[:, 0:D], ACT.Copy))
            do("dve", "hotw", ["hot"],
               lambda: dve.tensor_tensor(HOT[:, :, :], HOT[:, :, :],
                                         WEIGHT[:, :].unsqueeze(1).to_broadcast([P, BASES, PICKS]), ALU.mult))
            yield

            def q_product():
                for m in range(KD):
                    for k in range(KD):
                        last = pe.matmul(MA[:, D + m * P:D + (m + 1) * P], WQ_A[:, k, m * P:(m + 1) * P], XNT[:, k, :],
                                         start=k == 0, stop=k == KD - 1)
                return last

            do("pe", "q_ps", ["xt"], q_product)
            do("act", "qt", ["q_ps"], lambda: act.activation(QT[:, :, :].rearrange("p k t -> p (k t)"), MA[:, D:2 * D], ACT.Copy))

            def pack():
                with nc.allow_low_precision(reason="whole numbers below 2**24, summed in float32"):
                    return dve.tensor_reduce(PACKED[:, :], HOT[:, :, :], AX.X, ALU.add)

            do("dve", "packed", ["hotw"], pack)
            low = 2 ** DIGIT - 1
            for d in range(3):
                w = min(BASES, NPAD - d * BASES)
                if d == 0:
                    do("dve", "cut0", ["packed"], lambda: dve.tensor_scalar(
                        COUNTI[:, 0:w], PACKED[:, :], low, None, ALU.bitwise_and))
                else:
                    do("dve", f"cut{d}", [], lambda d=d: dve.tensor_scalar(
                        COUNTI[:, d * BASES:(d + 1) * BASES], PACKED[:, :], d * DIGIT, low,
                        ALU.logical_shift_right, ALU.bitwise_and))
            do("dve", "count", ["cut2", "<count_ps"], lambda: dve.tensor_copy(COUNT[:, :], COUNTI[:, :]))
            do("dve", "countr", ["<count_ps"],
               lambda: dve.tensor_copy(COUNTR[:, :, :], COUNTI[:, P:NPAD].unsqueeze(1).to_broadcast([P, GH, RPAD])))
            do("dve", "mask", ["count", "<scores_3"],
               lambda: dve.tensor_scalar(MASK[:, :], COUNT[:, 0:NKV], 0.0, MASKED, ALU.is_equal, ALU.mult))
            yield

            def count_transposes():
                pe.transpose(TA[:, 0:P], COUNT[:, 0:P], ident)
                return pe.transpose(TA[:, P:2 * P], COUNTR[:, :, :].rearrange("p h j -> p (h j)"), ident)

            do("pe", "count_ps", ["countr", "<x1"], count_transposes)
            do("act", "countt", ["count_ps", "<probs_3"],
               lambda: act.activation(COUNTT[:, :, :].rearrange("p k t -> p (k t)"), TA[:, 0:2 * P], ACT.Copy))
            yield
            for g in range(GROUPS):
                e = g % 2
                blk, row0 = g // 2, 64 * (g % 2)
                last_g = f"_{g - 1}"
                scores = SA[:, :, 0:2 * NKV].rearrange("p a (h j) -> p a h j", j=NKV)

                def score_products(blk=blk, row0=row0):
                    for i in range(2):
                        r = slice(row0 + 32 * i, row0 + 32 * i + 32)
                        pe.matmul(SA[:, i, 0:2 * NKV], QT[r, blk, :], KNOW[r, blk, :, :].rearrange("p a j -> p (a j)"),
                                  start=True, stop=False)
                    for i in range(2):
                        last = pe.matmul(SA[:, i, 0:2 * NKV], identb[:, :],
                                         MASK[:, :].unsqueeze(1).to_broadcast([P, 2, NKV]), start=False, stop=True)
                    return last

                do("pe", f"scores_{g}", ["know", "qt", "mask", f"shift{last_g}" if g else "<shift_3"], score_products)
                do("dve", f"max_{g}", [f"scores_{g}"],
                   lambda e=e: dve.tensor_reduce(MAXS[:, e, :].rearrange("p (a h) -> p a h", a=2), scores, AX.X, ALU.max))
                maxs = MAXS[:, e, :].rearrange("p (a h) -> p a h", a=2).unsqueeze(3)
                main = SHIFTED[:, e, 0:GH * P].rearrange("p (a h j) -> p a h j", a=2, h=2)
                rest = SHIFTED[:, e, GH * P:].rearrange("p (a h j) -> p a h j", a=2, h=2)[:, :, :, 0:REST]
                do("dve", f"shiftm_{g}", [f"max_{g}", f"exps_{g - 2}" if g > 1 else f"<exps_{g + 2}"],
                   lambda main=main, maxs=maxs: dve.tensor_tensor(
                       main, scores[:, :, :, 0:P], maxs.to_broadcast([P, 2, 2, P]), ALU.subtract))
                do("dve", f"shift_{g}", [],
                   lambda rest=rest, maxs=maxs: dve.tensor_tensor(
                       rest, scores[:, :, :, P:NKV], maxs.to_broadcast([P, 2, 2, REST]), ALU.subtract))
                do("act", f"exps_{g}", [f"shift_{g}", f"exps_ps_{g - 2}" if g > 1 else f"<exps_ps_{g + 2}"],
                   lambda e=e: act.activation(EXPS[:, e, :], SHIFTED[:, e, :], ACT.Exp))
                yield

                def exp_transposes(e=e):
                    for hh in range(GH):
                        pe.transpose(TA[:, hh * P:(hh + 1) * P], EXPS[:, e, hh * P:(hh + 1) * P], ident)
                    return pe.transpose(MA[:, 3 * P:4 * P], EXPS[:, e, GH * P:], ident)

                do("pe", f"exps_ps_{g}", [f"exps_{g}", "countt", "qt", f"probs{last_g}" if g else "<x1"], exp_transposes)
                do("dve", f"probr_{g}", [f"exps_ps_{g}", "countt", f"values{last_g}" if g else "<values_3"],
                   lambda: dve.tensor_tensor(PR[:, :], MA[:, 3 * P:4 * P], COUNTT[:, 1, :], ALU.mult))
                do("dve", f"probs_{g}", [],
                   lambda: dve.tensor_tensor(PT[:, :, :], TA[:, :].rearrange("p (h q) -> p h q", h=GH),
                                             COUNTT[:, 0, :].unsqueeze(1).to_broadcast([P, GH, P]), ALU.mult))
                yield

                def value_products(g=g):
                    c0 = g * GH * VW
                    pe.matmul(MA[:, c0:c0 + GH * VW], PR[:, :], VRNOW[:, c0:c0 + GH * VW], start=True, stop=False)
                    for hh in range(GH):
                        last = pe.matmul(MA[:, c0 + hh * VW:c0 + (hh + 1) * VW], PT[:, hh, :], VNOW[:, g * GH + hh, :],
                                         start=False, stop=hh == GH - 1)
                    return last

                do("pe", f"values_{g}", [f"probs_{g}", "vrnow"], value_products)
            yield
            attn = MA[:, 0:HA * VW].rearrange("p (h w) -> p h w", w=VW)
            do("dve", "rsum", ["values_3"],
               lambda: dve.reciprocal(RSUM[:, :].unsqueeze(2), attn[:, :, DA:VW]))
            do("dve", "on", ["rsum", "<ont_ps"],
               lambda: dve.tensor_tensor(ON[:, :].rearrange("p (h d) -> p h d", d=DA), attn[:, :, 0:DA],
                                         RSUM[:, :].unsqueeze(2).to_broadcast([P, HA, DA]), ALU.mult))
            do("pe", "ont_ps", ["on"], lambda: transposes(TA[:, :], ON[:, :], KD))
            do("act", "ont", ["ont_ps", "<y_ps"],
               lambda: act.activation(ONT[:, :, :].rearrange("p k t -> p (k t)"), TA[:, 0:D], ACT.Copy))
            yield

            def y_product():
                for k in range(KD):
                    last = pe.matmul(TA[:, D:2 * D], ONT[:, k, :], WOUT[:, k, :], start=k == 0, stop=k == KD - 1)
                return last

            do("pe", "y_ps", ["ont"], y_product)
            do("dve", "x1", ["y_ps", "load_xb", "<ffn.x1b", "<ffn.xm"],
               lambda: dve.tensor_tensor(X1[:, :], TA[:, D:2 * D], XB[:, :], ALU.add))
            yield

        def ffn(t):
            steps.begin("ffn", t)

            def do(engine, name, after, issue, dma=False, apart=False):
                steps.do("ffn", engine, name, after, issue, dma, apart)

            def transposes(bank, src, n):
                for k in range(n):
                    last = pe.transpose(bank[:, k * P:(k + 1) * P], src[:, k * P:(k + 1) * P], ident)
                return last

            def flat(a):
                return a[:, :, :].rearrange("p a b -> p (a b)")

            do("pool", "x1b", ["att.x1", "<out"], lambda: pool.tensor_copy(X1B[:, :], X1[:, :]), apart=True)
            do("dve", "stats", ["att.x1"], lambda: dve.bn_stats(STATS2[:, :], X1[:, :]))
            do("dve", "meanvar", ["stats"], lambda: dve.bn_aggr(MV2[:, :], STATS2[:, :]), apart=True)
            do("act", "lnvar", ["meanvar"], lambda: act.activation(RSTD2[:, 0:1], MV2[:, 1:2], ACT.Ln, bias=eps))
            do("act", "rstd", ["lnvar"], lambda: act.activation(RSTD2[:, 1:2], RSTD2[:, 0:1], ACT.Exp, scale=-0.5))
            do("dve", "xm", ["rstd"],
               lambda: dve.tensor_scalar(XM[:, :], X1[:, :], MV2[:, 0:1], RSTD2[:, 1:2], ALU.subtract, ALU.mult))
            do("pe", "xmt_ps", ["xm", "<out"], lambda: transposes(F[:, 0, :], XM[:, :], KD))
            do("act", "xmt", ["xmt_ps"], lambda: act.activation(flat(XMT), F[:, 0, 0:D], ACT.Copy))
            yield

            def hidden():
                for k in range(KD):
                    pe.matmul(F[:, 1, 0:NE], XMT[:, k, :], WE[:, k, :], start=k == 0, stop=k == KD - 1)
                for m in range(2):
                    for k in range(KD):
                        last = pe.matmul(F[:, 0, (2 + m) * P:(3 + m) * P], WA[:, k, m * P:(m + 1) * P], XMT[:, k, :],
                                         start=k == 0, stop=k == KD - 1)
                return last

            do("pe", "hidden_ps", ["xmt", "<ogt"], hidden)
            do("act", "logit", ["hidden_ps"], lambda: act.activation(LOGIT[:, :], F[:, 1, 0:NE], ACT.Copy))
            do("act", "hid2", [],
               lambda: act.activation(HID2[:, :], F[:, 0, 3 * P:4 * P], ACT.Identity, bias=const("onerow")))
            do("act", "hid1", [], lambda: act.activation(HID1[:, :], F[:, 0, 2 * P:3 * P], ACT.Copy))
            yield

            do("dve", "rmax", ["logit"], lambda: dve.tensor_reduce(RT[:, 0:1], LOGIT[:, :], AX.X, ALU.max))
            do("dve", "rnmax", [], lambda: dve.tensor_reduce(RT[:, 1:2], LOGIT[:, :], AX.X, ALU.max, negate=True))
            do("act", "rexp", ["rnmax"],
               lambda: act.activation(ELOG[:, :], LOGIT[:, :], ACT.Exp, bias=RT[:, 1:2]))
            do("dve", "rvals", ["rmax"],
               lambda: dve.scalar_tensor_tensor(VALS[:, :], LOGIT[:, :], RT[:, 0:1], prio, ALU.is_equal, ALU.mult))
            do("dve", "label", ["rvals"], lambda: dve.tensor_reduce(RT[:, 4:5], VALS[:, :], AX.X, ALU.max))
            do("dve", "labb", ["label"], lambda: dve.tensor_copy(LABB[:, :], RT[:, 4:5]))
            do("dve", "isexp", [],
               lambda: dve.tensor_scalar(ISEXP[:, :], prio, RT[:, 4:5], None, ALU.is_equal))
            do("dve", "halfe", ["isexp"],
               lambda: dve.tensor_tensor(HALFE[:, :, :], const("half").unsqueeze(2).to_broadcast([P, 2, NE]),
                                         ISEXP[:, :].unsqueeze(1).to_broadcast([P, 2, NE]), ALU.mult))
            do("dve", "rsum", ["rexp"], lambda: dve.tensor_reduce(RT[:, 2:3], ELOG[:, :], AX.X, ALU.add))
            do("dve", "rweight", ["rsum"], lambda: dve.reciprocal(RT[:, 3:4], RT[:, 2:3]))

            def gates():
                pe.matmul(F[:, 1, :], HID2[64:96, :], WGB[64:96, :], start=True, stop=True)
                pe.matmul(F[:, 2, :], HID2[96:128, :], WGB[96:128, :], start=True, stop=True)
                return pe.matmul(F[:, 3, :], HID2[0:64, :], WGB[0:64, :], start=True, stop=True)

            do("pe", "gates_ps", ["hid2", "<state2", "<state1"], gates)
            do("act", "gabs", ["gates_ps"], lambda: act.activation(SP3[:, :, :], F[:, 1:4, :], ACT.Abs))
            yield

            def v_product():
                for k in range(KD):
                    last = pe.matmul(F[:, 0, :], XMT[:, k, :], WV[:, k, :], start=k == 0, stop=k == KD - 1)
                return last

            do("pe", "v_ps", ["hid1"], v_product)
            do("act", "gexp", ["gabs"], lambda: act.activation(SP3[:, :, :], SP3[:, :, :], ACT.Exp, scale=-1.0))
            do("act", "v", ["v_ps", "<kv_ps"], lambda: act.activation(V[:, :], F[:, 0, :], ACT.Copy))
            do("act", "gln", ["gexp"], lambda: act.activation(SP3[:, :, :], SP3[:, :, :], ACT.Ln, bias=1.0))
            do("dve", "ls", ["gln"],
               lambda: dve.scalar_tensor_tensor(LS3[:, :, :], F[:, 1:4, :], 0.0, SP3[:, :, :], ALU.min, ALU.subtract))
            yield

            def router_rows():
                pe.matmul(F[:, 0, 0:P], RT[:, 3:4].to_broadcast([P, P]), ident, start=True, stop=True)
                return pe.matmul(F[:, 0, P:2 * P], LABB[:, 0:1].to_broadcast([P, P]), identb[:, :], start=True, stop=True)

            do("pe", "rows_ps", ["v", "labb", "rweight"], router_rows)
            do("dve", "hq", ["rows_ps"],
               lambda: dve.tensor_tensor(HQ[0:64, :], HID1[0:64, :], F[0:64, 0, 0:P], ALU.mult))
            label_row = F[:, 0, P:2 * P]
            do("dve", "cume", [],
               lambda: dve.scalar_tensor_tensor(CUME[:, :], label_row, RT[:, 4:5], cum, ALU.is_equal, ALU.mult))
            do("dve", "trie", [],
               lambda: dve.scalar_tensor_tensor(TRIE[:, :], label_row, RT[:, 4:5], tri, ALU.is_equal, ALU.mult))
            do("dve", "isexpt", ["<qm"],
               lambda: dve.tensor_tensor(ISEXPT[:, :, :], label_row.unsqueeze(1).to_broadcast([P, NE, P]),
                                         prio.unsqueeze(2).to_broadcast([P, NE, P]), ALU.is_equal))
            yield

            def by_pairs(bank, lhs, rhs, contraction=1):
                for p in range(NP):
                    for k in range(contraction):
                        last = pe.matmul(bank[:, p * P:(p + 1) * P], lhs(k, p), rhs(k), start=k == 0,
                                         stop=k == contraction - 1)
                return last

            def cols(p):
                return slice(p * P, (p + 1) * P)

            do("pe", "g1_ps", ["ls"], lambda: by_pairs(F[:, 1, :], lambda k, p: LS3[:, 0, cols(p)], lambda k: cum))
            do("act", "ep1", ["g1_ps"], lambda: act.activation(EP1[:, :], F[:, 1, :], ACT.Exp))
            do("act", "en1", [], lambda: act.activation(EN1[:, :], F[:, 1, :], ACT.Exp, scale=-1.0))
            do("pe", "q1_ps", [],
               lambda: by_pairs(F[:, 2, :], lambda k, p: WQ[:, k, cols(p)], lambda k: XMT[:, k, :], KD))
            do("dve", "q1", ["q1_ps", "en1", "<o_ps"],
               lambda: dve.scalar_tensor_tensor(QM[:, NE, :, :].rearrange("p a b -> p (a b)"), F[:, 2, :], DK ** -0.5,
                                                EP1[:, :], ALU.mult, ALU.mult))
            do("act", "sigm", ["ls"], lambda: act.activation(SG[:, :], LS3[:, 2, :], ACT.Exp))
            do("dve", "sg", ["sigm"], lambda: dve.tensor_tensor(SG[:, :], F[:, 3, :], SG[:, :], ALU.mult))
            yield
            do("pe", "k2_ps", ["isexpt"],
               lambda: pe.matmul(F[:, 0, :], HID1[64:128, :], WQKB[64:128, :], start=True, stop=True))
            k2p = F[:, 0, :].rearrange("p (h d) -> p h d", d=DK)
            do("dve", "k2max", ["k2_ps"], lambda: dve.tensor_reduce(KS[:, 0, :], k2p, AX.X, ALU.max))
            do("dve", "k2shift", ["k2max"],
               lambda: dve.tensor_tensor(K2[:, :, :], k2p, KS[:, 0, :].unsqueeze(2).to_broadcast([P, H, DK]), ALU.subtract))
            do("act", "k2exp", ["k2shift"], lambda: act.activation(K2[:, :, :], K2[:, :, :], ACT.Exp))
            do("pe", "k1_ps", ["sg"],
               lambda: by_pairs(F[:, 3, :], lambda k, p: WK[:, k, cols(p)], lambda k: XMT[:, k, :], KD))
            do("dve", "k1", ["k1_ps", "en1"],
               lambda: dve.tensor_tensor(flat(KG1T), F[:, 3, :], EN1[:, :], ALU.mult))
            yield
            do("dve", "k2sum", ["k2exp"], lambda: dve.tensor_reduce(KS[:, 1, :], K2[:, :, :], AX.X, ALU.add))
            do("dve", "k2rec", ["k2sum"], lambda: dve.reciprocal(KS[:, 2, :], KS[:, 1, :]))
            do("dve", "k2w", ["k2rec"],
               lambda: dve.tensor_scalar(KS[:, 3, :], KS[:, 2, :], RT[:, 3:4], None, ALU.mult))
            do("dve", "k2", ["k2w"],
               lambda: dve.tensor_tensor(K2[:, :, :], K2[:, :, :], KS[:, 3, :].unsqueeze(2).to_broadcast([P, H, DK]), ALU.mult))
            do("pe", "g2_ps", ["cume", "en1"],
               lambda: by_pairs(F[:, 1, :], lambda k, p: LS3[:, 1, cols(p)], lambda k: CUME[:, :]))
            do("act", "en2", ["g2_ps"], lambda: act.activation(EN2[:, :], F[:, 1, :], ACT.Exp, scale=-1.0))
            do("act", "ep2", [], lambda: act.activation(EP2[:, :], F[:, 1, :], ACT.Exp))
            do("pe", "q2_ps", ["q1", "hq"],
               lambda: by_pairs(F[:, 2, :], lambda k, p: WQKB[0:64, cols(p)], lambda k: HQ[0:64, :]))
            do("dve", "q2", ["q2_ps", "ep2", "<qm"],
               lambda: dve.scalar_tensor_tensor(flat(QG2), F[:, 2, :], DK ** -0.5, EP2[:, :], ALU.mult, ALU.mult))
            for e in range(NE):
                do("pool", "qm" if e == NE - 1 else f"qm{e}", ["q2", "<o_ps"],
                   lambda e=e: pool.tensor_tensor(QM[:, e, :, :], QG2[:, :, :],
                                                  ISEXPT[:, e, :].unsqueeze(1).to_broadcast([P, NP, P]), ALU.mult))
            yield
            do("pe", "k1t_ps", ["k1"], lambda: transposes(F[:, 3, :], flat(KG1T), NP))
            do("act", "kgm4", ["k1t_ps", "<kv_ps"], lambda: act.activation(KGM[:, NE, :], F[:, 3, :], ACT.Copy))
            do("pe", "k2t_ps", ["k2"], lambda: transposes(F[:, 0, :], K2[:, :, :].rearrange("p h d -> p (h d)"), NP))
            do("dve", "kg2", ["k2t_ps", "en2"],
               lambda: dve.tensor_tensor(flat(KG2T), F[:, 0, :], EN2[:, :], ALU.mult))
            yield

            def inner(banks, kt, q):
                for odd in range(2):
                    r = slice(64 * odd, 64 * odd + 64)
                    for p in range(NP):
                        last = pe.matmul(banks[odd][:, cols(p)], kt[r, p, :], q(r, p), start=True, stop=True)
                return last

            do("pe", "a1_ps", ["ep2", "q2"],
               lambda: inner((F[:, 1, :], F[:, 2, :]), KG1T, lambda r, p: QM[r, NE, p, :]))
            for odd in range(2):
                do("dve", f"at1_{odd}", ["a1_ps", "<o_ps"],
                   lambda odd=odd: dve.tensor_tensor(AT1[:, odd, :, :],
                                                     F[:, 1 + odd, :].rearrange("p (a b) -> p a b", b=P),
                                                     tri.unsqueeze(1).to_broadcast([P, NP, P]), ALU.mult))

            def half_sums():
                for p in range(NP):
                    o = F[:, 0, 0:2 * ST * NP].rearrange("p (a e q) -> p a e q", a=2, e=ST)[:, :, :, p]
                    pe.matmul(o[:, :, NE], LS3[:, 0, cols(p)], const("half"), start=True, stop=True)
                    last = pe.matmul(o[:, :, 0:NE], LS3[:, 1, cols(p)], HALFE[:, :, :], start=True, stop=True)
                return last

            do("pe", "sums_ps", ["kg2", "halfe"], half_sums)
            do("act", "eg", ["sums_ps", "<elast"],
               lambda: act.activation(EG[:, :, :, :].rearrange("p a e q -> p (a e q)"), F[:, 0, 0:2 * ST * NP], ACT.Exp))
            do("dve", "dec", ["eg", "<state3", "<decay"],
               lambda: dve.scalar_tensor_tensor(flat(DEC), flat(ELAST), CONST[:, bass.ds(_C["keep"][0] + t, 1)],
                                                EG[:, 0, :, :].rearrange("p e q -> p (e q)"), ALU.mult, ALU.mult))
            do("dve", "elast", ["dec"], lambda: dve.tensor_copy(ELAST[:, :, :], EG[:, 1, :, :]))
            do("pool", "decay", ["dec", "<state3"],
               lambda: pool.tensor_tensor(STATE[:, :, :, :].rearrange("p e q d -> p (e q) d"),
                                          STATE[:, :, :, :].rearrange("p e q d -> p (e q) d"),
                                          flat(DEC).unsqueeze(2).to_broadcast([P, ST * NP, DK]), ALU.mult))
            yield
            do("pe", "kg2t_ps", ["kgm4", "kg2"], lambda: transposes(F[:, 3, :], flat(KG2T), NP))
            for e in range(NE):
                do("act", f"kgm{e}", ["kg2t_ps", "isexp", "<kv_ps"],
                   lambda e=e: act.activation(KGM[:, e, :], F[:, 3, :], ACT.Copy, scale=ISEXP[:, e:e + 1]))
            do("pe", "a2_ps", [f"kgm{NE - 1}", "eg"],
               lambda: inner((F[:, 0, :], F[:, 3, :]), KG2T, lambda r, p: QG2[r, p, :]))
            for odd in range(2):
                do("dve", f"at2_{odd}", ["a2_ps", "trie", "<o_ps"],
                   lambda odd=odd: dve.tensor_tensor(AT2[:, odd, :, :],
                                                     F[:, 3 * odd, :].rearrange("p (a b) -> p a b", b=P),
                                                     TRIE[:, :].unsqueeze(1).to_broadcast([P, NP, P]), ALU.mult))
            yield

            def inner_outputs():
                for n, at in enumerate((AT1, AT2)):
                    for h in range(H):
                        c = slice(h * DK, (h + 1) * DK)
                        last = pe.matmul(F[:, 1, c], at[:, h % 2, h // 2, :], V[:, c], start=n == 0 and h == 0,
                                         stop=False, skip_group_check=True)
                return last

            def state_outputs(odd):
                r = slice(64 * odd, 64 * odd + 64)
                for p in range(NP):
                    c = slice((2 * p + odd) * DK, (2 * p + odd + 1) * DK)
                    for e in range(ST):
                        last = pe.matmul(F[:, 1, c], QM[r, e, p, :], STATE[r, e, p, :], start=False,
                                         stop=odd == 1 and p == NP - 1 and e == ST - 1, skip_group_check=True)
                return last

            def kv_products():
                for e in range(ST):
                    bank, c0 = (0, 2, 3)[e // 2], (e % 2) * NP * DK
                    for h in range(H):
                        c = slice(h * DK, (h + 1) * DK)
                        last = pe.matmul(F[64 * (h % 2):64 * (h % 2) + 64, bank, c0 + (h // 2) * DK:c0 + (h // 2 + 1) * DK],
                                         KGM[:, e, c], V[:, c], start=True, stop=True)
                return last

            do("pe", "kv_ps", ["at1_1", "at2_1"], kv_products)
            do("pe", "o_inner", [], inner_outputs)
            do("pe", "o_even", ["decay", "qm"], lambda: state_outputs(0))
            do("pe", "o_ps", ["o_even"], lambda: state_outputs(1))
            yield
            for n, (bank, e0, e1) in enumerate(((0, 0, 2), (2, 2, 4), (3, 4, 5))):
                state = STATE[:, e0:e1, :, :].rearrange("p e q d -> p (e q d)")
                do("dve", f"state{n + 1}", ["o_ps", "kv_ps"],
                   lambda bank=bank, state=state: dve.tensor_tensor(
                       state, state, F[:, bank, 0:state.shape[1]], ALU.add))
            o = F[:, 1, :].rearrange("p (h d) -> p h d", d=DK)
            do("act", "sq", ["o_ps"], lambda: act.activation(SQ[:, :, :], o, ACT.Square))
            do("dve", "ms", ["sq"], lambda: dve.tensor_reduce(RMS[:, 0, :], SQ[:, :, :], AX.X, ALU.add))
            do("act", "lnms", ["ms"],
               lambda: act.activation(RMS[:, 0, :], RMS[:, 0, :], ACT.Ln, bias=eps, scale=1.0 / DK))
            do("act", "rms", ["lnms"], lambda: act.activation(RMS[:, 1, :], RMS[:, 0, :], ACT.Exp, scale=-0.5))
            yield
            do("dve", "onorm", ["rms"],
               lambda: dve.tensor_tensor(OG[:, :, :], o, RMS[:, 1, :].unsqueeze(2).to_broadcast([P, H, DK]), ALU.mult))
            do("pool", "og", ["onorm", "sg"],
               lambda: pool.tensor_tensor(flat(OG), flat(OG), SG[:, :], ALU.mult))
            do("pe", "ogt_ps", ["og", "onorm"], lambda: transposes(F[:, 1, :], flat(OG), NP))
            do("act", "ogt", ["ogt_ps"], lambda: act.activation(flat(OGT), F[:, 1, :], ACT.Copy))
            yield

            def out_product():
                for p in range(NP):
                    last = pe.matmul(F[:, 0, 0:D], OGT[:, p, :], WO[:, p, :], start=p == 0, stop=p == NP - 1)
                return last

            do("pe", "y_ps", ["ogt", "state1"], out_product)
            do("dve", "out", ["y_ps", "x1b", "<store"],
               lambda: dve.tensor_tensor(OUT[:, :], F[:, 0, 0:D], X1B[:, :], ALU.add))
            do("sp", "store", ["out"], lambda: sp.dma_start(out[bass.ts(t, P), :], OUT[:, :]), dma=True)
            yield

        def both(a, b):
            live = [g for g in (a, b) if g is not None]
            while live:
                for g in list(live):
                    if next(g, "end") == "end":
                        live.remove(g)

        both(att(0), ffn(0))
        steps.dry = False
        both(att(0), None)
        both(att(1), ffn(0))
        with nc.Fori(2, TILES) as t:
            both(att(t), ffn(t - 1))
        both(None, ffn(TILES - 1))
        steps.wait("ffn", "sp", "store")


def kernel(**inputs):
    import concourse.bacc as bacc
    from concourse.bass_utils import run_bass_kernel_spmd

    def a(name):
        return np.asarray(inputs[name])

    def blocks(w):
        return np.ascontiguousarray(w.reshape(-1, P, w.shape[1]).transpose(1, 0, 2))

    f = "L0_ffn_"
    pad = np.zeros((D, 16), np.float32)
    gap = np.zeros((15, HD), np.float32)
    arrays = {
        "x": a("x").reshape(B * L, D),
        "idx": a("itok_BxSx64_0_2047").reshape(B * L, PICKS),
        "ctxT": blocks(a("ctx_1024").reshape(B * NKV, D).T),
        "consts": constants(),
        "w_q": blocks(a("L0_xattn_W_q").T),
        "w_down": blocks(a("L0_xattn_W_kv_down").T),
        "w_up": a("L0_xattn_W_kv_up").T,
        "w_out": blocks(a("L0_xattn_W_out").T),
        "wa": blocks(np.concatenate([a(f + "Wqa"), a(f + "Wka"), a(f + "Wga"), a(f + "Wg1a"), pad, a(f + "Wg2a"), pad], 1)),
        "we": blocks(a(f + "We")),
        "wq": blocks(a(f + "Wq")),
        "wk": blocks(a(f + "Wk")),
        "wv": blocks(a(f + "Wv")),
        "wqk_b": np.concatenate([a(f + "Wqb"), a(f + "Wkb")]),
        "wg_b": np.concatenate([a(f + "Wgb"), a(f + "Wg1b"), a(f + "bg1")[None], gap, a(f + "Wg2b"), a(f + "bg2")[None], gap]),
        "wo": blocks(a(f + "Wo")),
        "norm_w": np.concatenate([a(f + "norm_w"), a(f + "norm_w")])[:, None],
    }
    nc = bacc.Bacc("TRN2", target_bir_lowering=False, num_devices=1)
    args, fed = [], {}
    for name, v in arrays.items():
        v = np.ascontiguousarray(v)
        fed[name + "_dram"] = v
        args.append(nc.dram_tensor(name + "_dram", v.shape, mybir.dt.from_np(v.dtype), kind="ExternalInput").ap())
    out = nc.dram_tensor("out_dram", (B * L, D), mybir.dt.float32, kind="ExternalOutput").ap()
    program(nc, *args, out)
    r = run_bass_kernel_spmd(nc, [fed], core_ids=[0])
    return r.results[0]["out_dram"].reshape(B, L, D)
```

```python
import numpy as np
import concourse.bass as bass
from concourse import mybir
from contextlib import ExitStack

P = 128
B, L, D = 4, 1024, 256
TILES = B * L // P
TPB = L // P
KD = D // P
NKV, PICKS = 154, 64
HA, DA = 16, 16
REST = NKV - P
RPAD, NPAD = 32, 160
BASES, DIGIT = 52, 7
GROUPS, GH = 4, 4
VW = 32
KW = KD * 2 * NKV
KVW = KW + 2 * HA * VW
H, DK = 8, 64
HD = H * DK
NP = HD // P
NE = 4
ST = NE + 1
NORMALIZER = 16.0
EPS = 1e-5
MASKED = -1e30

_C = {}
_n = 0
for _name, _w in (("ident", P), ("cum", P), ("tri", P), ("half", 2), ("prio", NE), ("onerow", 1), ("eps", 1), ("pairs", P),
                  ("bases", BASES), ("even_odd", 2), ("quarter", GH), ("keep", TILES)):
    _C[_name] = (_n, _n + _w)
    _n += _w
NCONST = _n


def constants():
    c = np.zeros((P, NCONST), np.float32)
    r = np.arange(P)
    s, t = r[:, None], r[None, :]
    mid = P // 2

    def put(name, v):
        c[:, _C[name][0]:_C[name][1]] = v

    put("ident", s == t)
    put("cum", (((s >= mid) & (s <= t)) * 1.0 - ((s < mid) & (s > t)) * 1.0) / NORMALIZER)
    put("tri", s <= t)
    put("half", np.stack([r < mid, r >= mid], 1) / NORMALIZER)
    put("prio", np.arange(NE, 0, -1)[None, :])
    put("onerow", ((r == 80) | (r == 112))[:, None])
    put("eps", EPS)
    put("pairs", (s // DK == t // DK) / DK)
    put("bases", np.arange(BASES)[None, :])
    put("even_odd", np.stack([(r // DA) % 2 == 0, (r // DA) % 2 == 1], 1) * DA ** -0.5)
    put("quarter", (r // RPAD)[:, None] == np.arange(GH)[None, :])
    put("keep", (np.arange(TILES) % TPB != 0)[None, :])
    return c


TURNS = "AAACACACAA" "CC" "AA" "CCCACCCACCCACCC" "AA" "CACCCCC"


class Steps:

    def __init__(self, nc, ctx):
        self.nc, self.ctx = nc, ctx
        self.engines = {"pe": nc.tensor, "dve": nc.vector, "act": nc.scalar, "pool": nc.gpsimd, "sp": nc.sync}
        self.gate = ctx.enter_context(nc.semaphore("gate"))
        self.sems, self.total, self.number = {}, {}, {}
        self.dry = True
        self.tile = {}
        self.waited = {}

    def begin(self, part, tile, first):
        self.tile[part] = tile, first
        for key in [k for k in self.waited if k[0] == part]:
            del self.waited[key]

    def do(self, part, engine, name, after, issue, dma=False, apart=False):
        lane = (part, name if dma else engine)
        if self.dry:
            self.total[lane] = self.total.get(lane, 0) + 1
            if lane not in self.sems:
                self.sems[lane] = self.ctx.enter_context(self.nc.semaphore("done_" + "_".join(lane)))
            self.number[f"{part}.{name}"] = (lane, self.total[lane], 16 if dma else 1)
            return
        for a in after:
            self.wait(part, engine, a)
        if apart and after:
            self.engines[engine].sem_inc(self.gate, 1)
        issue().then_inc(self.sems[lane], 16 if dma else 1)

    def wait(self, part, engine, what):
        name = what.lstrip("<>")
        back = what.count("<") - what.count(">")
        if "." not in name:
            name = f"{part}.{name}"
        lane, number, unit = self.number[name]
        tile, first = self.tile[part]
        if first < back or isinstance(tile, int) and tile - back >= TILES:
            return
        number -= self.total[lane] * back
        if number <= self.waited.get((part, engine, lane), -10 ** 9):
            return
        self.waited[(part, engine, lane)] = number
        self.engines[engine].wait_ge(self.sems[lane], (tile * self.total[lane] + number) * unit)


def program(nc, x, idx, ctxT, consts, w_q, w_down, w_up, w_out, wa, we, wq, wk, wv, wqk_b, wg_b, wo, norm_w, out):
    f32, bf16, i32 = mybir.dt.float32, mybir.dt.bfloat16, mybir.dt.int32
    ALU, ACT, AX = mybir.AluOpType, mybir.ActivationFunctionType, mybir.AxisListType
    pe, dve, act, pool, sp = nc.tensor, nc.vector, nc.scalar, nc.gpsimd, nc.sync

    with ExitStack() as ctx:
        def sb(name, shape, dt=f32):
            return ctx.enter_context(nc.sbuf_tensor(name, shape, dt))

        def ps(name, shape):
            return ctx.enter_context(nc.psum_tensor(name, shape, f32))

        def sem(name):
            return ctx.enter_context(nc.semaphore(name))

        CONST = sb("CONST", [P, NCONST])

        def const(name):
            return CONST[:, _C[name][0]:_C[name][1]]

        ident, cum, tri = const("ident"), const("cum"), const("tri")
        prio, eps = const("prio"), const("eps")
        WQ_A = sb("WQ_A", [P, KD, D])
        WOUT = sb("WOUT", [P, KD, D])
        WA = sb("WA", [P, KD, 256])
        WE = sb("WE", [P, KD, NE])
        WQ = sb("WQ", [P, KD, HD])
        WK = sb("WK", [P, KD, HD])
        WV = sb("WV", [P, KD, HD])
        WQKB = sb("WQKB", [P, HD])
        WGB = sb("WGB", [P, HD])
        WO = sb("WO", [P, NP, D])
        NORMW = sb("NORMW", [P, 1])
        identb = sb("identb", [P, P], bf16)
        BASETAB = sb("BASETAB", [P, BASES, PICKS], bf16)

        SA = ps("SA", [P, 2, 512])
        TA = ps("TA", [P, 512])
        MA = ps("MA", [P, 512])
        F = ps("F", [P, 4, 512])

        s_w = sem("s_w")
        s_pe0 = sem("s_pe0")
        s_dve0 = sem("s_dve0")
        s_act0 = sem("s_act0")
        s_kv = sem("s_kv")
        steps = Steps(nc, ctx)

        brief = ExitStack()

        def brief_sb(name, shape):
            return brief.enter_context(nc.sbuf_tensor(name, shape, f32))

        WDOWN = brief_sb("WDOWN", [P, KD, P])
        WUP = brief_sb("WUP", [P, 2 * D])
        CTXT = brief_sb("CTXT", [P, KD, B * NKV])
        CT = brief_sb("CT", [P, B, NKV])
        CREST = brief_sb("CREST", [P, B, GH, RPAD])
        KALL = brief_sb("KALL", [P, B, KD, 2, NKV])
        VALL = brief_sb("VALL", [P, B, HA, VW])
        VRALL = brief_sb("VRALL", [P, B, GROUPS * GH * VW])
        kv_dram = nc.dram_tensor("kv_dram", (B * P, KVW), f32).ap()
        loads = [(CONST[:, :], consts), (CTXT[:, :, :], ctxT), (WDOWN[:, :, :], w_down), (WUP[:, :], w_up),
                 (WQ_A[:, :, :], w_q), (WOUT[:, :, :], w_out), (WA[:, :, :], wa), (WE[:, :, :], we),
                 (WQ[:, :, :], wq), (WK[:, :, :], wk), (WV[:, :, :], wv), (WQKB[:, :], wqk_b), (WGB[:, :], wg_b),
                 (WO[:, :, :], wo), (NORMW[:, :], norm_w)]
        for n, (dst, src) in enumerate(loads):
            (sp if n % 2 == 0 else act).dma_start(dst, src).then_inc(s_w, 16)
        act.preload_act_table_set("natural_log_exp_and_others")
        pool.memset(VALL[:, :, :, :], 0.0)
        pool.memset(VRALL[:, :, :], 0.0)
        pool.memset(CREST[:, :, :, :], 0.0).then_inc(s_act0, 1)
        for e in (pe, dve, act, pool):
            e.wait_ge(s_w, 16 * len(loads))
        half = 2 * NKV
        for c in range(2):
            for k in range(KD):
                last = pe.matmul(F[:, c, 0:half], WDOWN[:, k, :], CTXT[:, k, c * half:(c + 1) * half],
                                 start=k == 0, stop=k == KD - 1)
        last.then_inc(s_pe0, 1)
        dve.wait_ge(s_pe0, 1)
        CTf = CT[:, :, :].rearrange("p b j -> p (b j)")
        for c in range(2):
            last = dve.tensor_copy(CTf[:, c * half:(c + 1) * half], F[:, c, 0:half])
        last.then_inc(s_dve0, 1)
        dve.wait_ge(s_dve0, 1)
        dve.wait_ge(s_act0, 1)
        for hh in range(GH):
            last = dve.tensor_copy(CREST[:, :, hh, 0:REST], CT[:, :, P:NKV])
        last.then_inc(s_dve0, 1)
        pe.wait_ge(s_dve0, 1)
        for blk in range(KD):
            for c in range(2):
                bank = SA[:, c, 0:half] if blk == 0 else (TA, MA)[c][:, 0:half]
                last = pe.matmul(bank, WUP[:, blk * P:(blk + 1) * P], CTf[:, c * half:(c + 1) * half],
                                 start=True, stop=True)
        last.then_inc(s_pe0, 1)
        dve.wait_ge(s_pe0, 2)
        for blk in range(KD):
            for c in range(2):
                bank = SA[:, c, 0:half] if blk == 0 else (TA, MA)[c][:, 0:half]
                for odd in range(2):
                    dve.tensor_scalar(KALL[:, 2 * c:2 * c + 2, blk, odd, :],
                                      bank.rearrange("p (b j) -> p b j", b=2),
                                      const("even_odd")[:, odd:odd + 1], None, ALU.mult)
        pe.wait_ge(s_dve0, 2)
        for b in range(B):
            pe.matmul(F[:, b, 0:D], CT[:, b, 0:P], WUP[:, D:2 * D], start=True, stop=True)
            last = pe.matmul(F[:, b, D:2 * D], CREST[:, b, :, :].rearrange("p h j -> p (h j)"), WUP[:, D:2 * D], start=True, stop=True)
        last.then_inc(s_pe0, 1)
        dve.wait_ge(s_pe0, 3)
        dve.memset(VALL[:, :, :, DA:DA + 1], 1.0)
        VR5 = VRALL[:, :, :].rearrange("p b (g h w) -> p b g h w", g=GROUPS, h=GH)
        for b in range(B):
            dve.tensor_copy(VALL[:, b, :, 0:DA], F[:, b, 0:D].rearrange("p (h d) -> p h d", d=DA))
            rest = F[:, b, D:2 * D].rearrange("p (g h d) -> p g h d", g=GROUPS, h=GH)
            for hh in range(GH):
                quarter = const("quarter")[:, hh:hh + 1]
                dve.tensor_scalar(VR5[:, b, :, hh, 0:DA], rest[:, :, hh, :], quarter, None, ALU.mult)
                dve.tensor_copy(VR5[:, b, :, hh, DA:DA + 1], quarter.unsqueeze(1).to_broadcast([P, GROUPS, 1]))
        for p in range(NP):
            dve.tensor_scalar(WO[:, p, :], WO[:, p, :], NORMW[:, 0:1], None, ALU.mult)
        dve.tensor_copy(identb[:, :], ident)
        last = dve.tensor_copy(BASETAB[:, :, :], const("bases").unsqueeze(2).to_broadcast([P, BASES, PICKS]))
        last.then_inc(s_dve0, 1)
        sp.wait_ge(s_dve0, 3)
        kv_rows = kv_dram.rearrange("(b p) w -> p b w", p=P)
        parts = ((0, KALL[:, :, :, :, :].rearrange("p b k a j -> p b (k a j)")),
                 (KW, VALL[:, :, :, :].rearrange("p b h w -> p b (h w)")), (KW + HA * VW, VRALL[:, :, :]))
        for c0, src in parts:
            sp.dma_start(kv_rows[:, :, c0:c0 + src.shape[2]], src).then_inc(s_kv, 16)
        sp.wait_ge(s_kv, 16 * len(parts))
        nc.all_engine_barrier()
        brief.close()

        def two(name, shape, dt=f32):
            return [sb(f"{name}{i}", shape, dt) for i in range(2)]

        KVNOW = two("KVNOW", [P, KVW])

        XA = sb("XA", [P, D])
        IDX = sb("IDX", [P, PICKS], i32)
        IW = [sb(f"IW{i}", [P, PICKS]) for i in range(6)]
        BASE = sb("BASE", [P, PICKS], bf16)
        WEIGHT = sb("WEIGHT", [P, PICKS], bf16)
        HOT = sb("HOT", [P, BASES, PICKS], bf16)
        PACKED = sb("PACKED", [P, BASES], i32)
        COUNTI = sb("COUNTI", [P, NPAD], i32)
        COUNT = sb("COUNT", [P, NPAD])
        COUNTR = sb("COUNTR", [P, GH, RPAD])
        STATS = sb("STATS", [P, 6])
        MV = sb("MV", [P, 2])
        RSTD = sb("RSTD", [P, 2])
        XN = sb("XN", [P, D])
        XNT = sb("XNT", [P, KD, P])
        MASKS = two("MASK", [P, NKV], bf16)
        COUNTTS = two("COUNTT", [P, 2, P])
        QTS = two("QT", [P, KD, P])

        XB = sb("XB", [P, D])
        MAXS = sb("MAXS", [P, 2, GH])
        SHIFTED = sb("SHIFTED", [P, 2, GH * NPAD])
        EXPS = sb("EXPS", [P, 2, GH * NPAD])
        PT = two("PT", [P, GH, P])
        PR = two("PR", [P, P])
        OT = sb("OT", [P, GROUPS, P])
        RSUM = sb("RSUM", [P, HA])
        ON = sb("ON", [P, D])
        ONT = sb("ONT", [P, KD, P])
        X1S = two("X1", [P, D])

        STATS2 = sb("STATS2", [P, 6])
        MV2 = sb("MV2", [P, 2])
        RSTD2 = sb("RSTD2", [P, 2])
        XM = sb("XM", [P, D])
        HID1 = sb("HID1", [P, P])
        HID2 = sb("HID2", [P, P])
        LOGIT = sb("LOGIT", [P, NE])
        RT = sb("RT", [P, 8])
        VALS = sb("VALS", [P, NE])
        ELOG = sb("ELOG", [P, NE])
        ISEXP = sb("ISEXP", [P, NE])
        LABB = sb("LABB", [P, 1], bf16)
        ZABS = sb("ZABS", [P, 3, HD])
        ZG = sb("ZG", [P, HD])
        KS = sb("KS", [P, 4, H])
        X1BS = two("X1B", [P, D])
        XMTS = two("XMT", [P, KD, P])
        HQS = two("HQ", [P, P])
        HALFES = two("HALFE", [P, 2, NE])
        CUMES = two("CUME", [P, P])
        TRIES = two("TRIE", [P, P])
        ISEXPTS = two("ISEXPT", [P, NE, P])
        LS3S = two("LS3_", [P, 3, HD])
        SGS = two("SG", [P, HD])
        VS = two("V", [P, HD])
        VMS = two("VM", [P, H, NE, DK])
        K2S = two("K2_", [P, H, DK])

        EP1 = sb("EP1", [P, HD])
        EN1 = sb("EN1", [P, HD])
        EP2 = sb("EP2", [P, HD])
        EN2 = sb("EN2", [P, HD])
        KG1T = sb("KG1T", [P, NP, P])
        KG2T = sb("KG2T", [P, NP, P])
        QG2 = sb("QG2", [P, NP, P])
        QM = sb("QM", [P, ST, NP, P])
        KG1 = sb("KG1", [P, HD])
        KG2 = sb("KG2", [P, HD])
        AT1 = sb("AT1", [P, 2, NP, P])
        AT2 = sb("AT2", [P, 2, NP, P])
        EG = sb("EG", [P, 2, NP, ST])
        ELAST = sb("ELAST", [P, NP, ST])
        DEC = sb("DEC", [P, NP, ST])
        STATE = sb("STATE", [P, NP, NE, DK])
        STATED = sb("STATED", [P, NP, DK])
        RMS = sb("RMS", [P, HD])
        OG = sb("OG", [P, NP, P])
        OUTS = two("OUT", [P, D])

        pool.memset(COUNTI[:, :], 0)
        pool.memset(SHIFTED[:, :, :], 0.0)
        pool.memset(STATE[:, :, :, :], 0.0)
        pool.memset(STATED[:, :, :], 0.0)
        pool.memset(ELAST[:, :, :], 0.0)
        nc.all_engine_barrier()

        def transposes(bank, src, n):
            for k in range(n):
                last = pe.transpose(bank[:, k * P:(k + 1) * P], src[:, k * P:(k + 1) * P], ident)
            return last

        def flat(a):
            return a.rearrange("p a b -> p (a b)")

        def starter(part):
            def begin(t, first):
                steps.begin(part, t, first)

                def do(engine, name, after, issue, dma=False, apart=False):
                    steps.do(part, engine, name, after, issue, dma, apart)
                return do
            return begin

        begin_a, begin_b, begin_c, begin_d = (starter(x) for x in "ABCD")
        spare = [F[:, 0, i * P:(i + 1) * P] for i in range(2)]
        spares = F[:, 0, 0:D].rearrange("p (k t) -> p k t", k=KD)

        def part_a(t, odd, first):
            do = begin_a(t, first)
            MASK, COUNTT, QT = MASKS[odd], COUNTTS[odd], QTS[odd]
            rows = bass.ts(t, P)
            do("sp", "load_idx", ["<idx_float"], lambda: sp.dma_start(IDX[:, :], idx[rows, :]), dma=True)
            do("sp", "load_xa", ["<xn"], lambda: sp.dma_start(XA[:, :], x[rows, :]), dma=True)
            yield
            do("pool", "idx_float", ["load_idx", "<idx_clamp"], lambda: pool.tensor_copy(IW[1][:, :], IDX[:, :]),
               apart=True)
            do("pool", "idx_wrap1", ["idx_float"],
               lambda: pool.tensor_scalar(IW[0][:, :], IW[1][:, :], 0.0, float(NKV), ALU.is_lt, ALU.mult), apart=True)
            do("pool", "idx_wrap2", ["idx_wrap1"],
               lambda: pool.tensor_tensor(IW[1][:, :], IW[1][:, :], IW[0][:, :], ALU.add))
            do("pool", "idx_clamp", ["idx_wrap2", "<weight"],
               lambda: pool.tensor_scalar(IW[2][:, :], IW[1][:, :], float(NKV - 1), 0.0, ALU.min, ALU.max), apart=True)
            do("pool", "digit1", ["idx_clamp"],
               lambda: pool.tensor_scalar(IW[3][:, :], IW[2][:, :], float(BASES), None, ALU.is_ge), apart=True)
            do("pool", "digit2", [],
               lambda: pool.tensor_scalar(IW[4][:, :], IW[2][:, :], float(2 * BASES), None, ALU.is_ge))
            yield
            do("dve", "stats", ["load_xa"], lambda: dve.bn_stats(STATS[:, :], XA[:, :]))
            do("dve", "meanvar", ["stats"], lambda: dve.bn_aggr(MV[:, :], STATS[:, :]), apart=True)
            yield
            do("act", "lnvar", ["meanvar"], lambda: act.activation(RSTD[:, 0:1], MV[:, 1:2], ACT.Ln, bias=eps))
            do("act", "rstd", ["lnvar"], lambda: act.activation(RSTD[:, 1:2], RSTD[:, 0:1], ACT.Exp, scale=-0.5))
            yield
            do("dve", "digits", ["digit2"],
               lambda: dve.tensor_tensor(IW[5][:, :], IW[3][:, :], IW[4][:, :], ALU.add))
            do("dve", "weight1", ["digits"],
               lambda: dve.tensor_scalar(IW[3][:, :], IW[3][:, :], float(2 ** DIGIT - 1), 1.0, ALU.mult, ALU.add))
            do("dve", "base", [],
               lambda: dve.scalar_tensor_tensor(BASE[:, :], IW[5][:, :], float(-BASES), IW[2][:, :], ALU.mult, ALU.add))
            do("dve", "weight", ["weight1"],
               lambda: dve.scalar_tensor_tensor(WEIGHT[:, :], IW[4][:, :], float(4 ** DIGIT - 2 ** DIGIT), IW[3][:, :],
                                                ALU.mult, ALU.add))
            do("dve", "xn", ["rstd", "<xt_ps"],
               lambda: dve.tensor_scalar(XN[:, :], XA[:, :], MV[:, 0:1], RSTD[:, 1:2], ALU.subtract, ALU.mult))
            yield
            do("dve", "hot", ["weight"],
               lambda: dve.tensor_tensor(HOT[:, :, :], BASE[:, :].unsqueeze(1).to_broadcast([P, BASES, PICKS]),
                                         BASETAB[:, :, :], ALU.is_equal))

            def xt_transposes():
                pe.transpose(spare[0], XN[:, 0:P], ident)
                return pe.transpose(spare[1], XN[:, P:2 * P], ident)

            do("pe", "xt_ps", ["xn", "<countt", "<<<C.k2shift"], xt_transposes)
            yield
            do("act", "xt", ["xt_ps", "<q_ps"], lambda: act.activation(XNT[:, :, :], spares, ACT.Copy))
            yield

            def q_product():
                for m in range(KD):
                    for k in range(KD):
                        last = pe.matmul(spare[m], WQ_A[:, k, m * P:(m + 1) * P], XNT[:, k, :],
                                         start=k == 0, stop=k == KD - 1)
                return last

            do("pe", "q_ps", ["xt", "<<C.xmt"], q_product)
            do("dve", "hotw", ["hot"],
               lambda: dve.tensor_tensor(HOT[:, :, :], HOT[:, :, :],
                                         WEIGHT[:, :].unsqueeze(1).to_broadcast([P, BASES, PICKS]), ALU.mult))
            yield
            do("act", "qt", ["q_ps", "<<B.scores_3"], lambda: act.activation(QT[:, :, :], spares, ACT.Copy))
            yield

            def pack(r):
                with nc.allow_low_precision(reason="whole numbers below 2**24, summed in float32"):
                    return dve.tensor_reduce(PACKED[:, r], HOT[:, r, :], AX.X, ALU.add)

            do("dve", "packed0", ["hotw"], lambda: pack(slice(0, BASES // 2)))
            yield
            do("dve", "packed", [], lambda: pack(slice(BASES // 2, BASES)))
            yield
            low = 2 ** DIGIT - 1
            do("dve", "cut0", ["packed"], lambda: dve.tensor_scalar(
                COUNTI[:, 0:BASES], PACKED[:, :], low, None, ALU.bitwise_and))
            for d in range(1, 3):
                do("dve", f"cut{d}", [], lambda d=d: dve.tensor_scalar(
                    COUNTI[:, d * BASES:(d + 1) * BASES], PACKED[:, :], d * DIGIT, low,
                    ALU.logical_shift_right, ALU.bitwise_and))
            do("dve", "count", ["cut2", "<count_ps"], lambda: dve.tensor_copy(COUNT[:, :], COUNTI[:, :]))
            do("dve", "countr", [],
               lambda: dve.tensor_copy(COUNTR[:, :, :], COUNTI[:, P:NPAD].unsqueeze(1).to_broadcast([P, GH, RPAD])))
            do("dve", "mask", ["count", "<<B.scores_3"],
               lambda: dve.tensor_scalar(MASK[:, :], COUNT[:, 0:NKV], 0.0, MASKED, ALU.is_equal, ALU.mult))
            yield

            def count_transposes():
                pe.transpose(spare[0], COUNT[:, 0:P], ident)
                return pe.transpose(spare[1], COUNTR[:, :, :].rearrange("p h j -> p (h j)"), ident)

            do("pe", "count_ps", ["countr", "qt", "<<C.isexpt"], count_transposes)
            yield
            do("act", "countt", ["count_ps", "<<B.probs_3"], lambda: act.activation(COUNTT[:, :, :], spares, ACT.Copy))
            yield

        def part_b(t, odd, first):
            do = begin_b(t, first)
            MASK, COUNTT, QT, X1 = MASKS[odd], COUNTTS[odd], QTS[odd], X1S[odd]
            KV = KVNOW[odd]
            KN, VN, VR = KV[:, 0:KW], KV[:, KW:KW + HA * VW], KV[:, KW + HA * VW:KVW]
            do("sp", "load_xb", ["<x1"], lambda: sp.dma_start(XB[:, :], x[bass.ts(t, P), :]), dma=True)
            do("sp", "kvnow", ["<scores_0"], lambda: sp.dma_start(KV[:, :], kv_dram[bass.ts(t // TPB, P), :]), dma=True)
            scores = SA[:, :, 0:2 * NKV].rearrange("p a (h j) -> p a h j", j=NKV)

            def before(name, g, back):
                return f"{name}_{g - back}" if g >= back else f"<{name}_{g - back + GROUPS}"

            def score_products(g):
                row0, blk = 64 * (g % 2), g // 2
                keys = KN[:, blk * 2 * NKV:(blk + 1) * 2 * NKV]
                for i in range(2):
                    r = slice(row0 + 32 * i, row0 + 32 * i + 32)
                    pe.matmul(SA[:, i, 0:2 * NKV], QT[r, blk, :], keys[r, :], start=True, stop=False)
                for i in range(2):
                    last = pe.matmul(SA[:, i, 0:2 * NKV], identb[:, :],
                                     MASK[:, :].unsqueeze(1).to_broadcast([P, 2, NKV]), start=False, stop=True)
                return last

            def exp_transposes(e):
                for hh in range(GH):
                    pe.transpose(TA[:, hh * P:(hh + 1) * P], EXPS[:, e, hh * P:(hh + 1) * P], ident)
                return pe.transpose(MA[:, 3 * P:4 * P], EXPS[:, e, GH * P:], ident)

            def value_products(g):
                o = MA[:, 0:P]
                pe.matmul(o, VR[:, g * P:(g + 1) * P], PR[g % 2][:, :], start=True, stop=False, skip_group_check=True)
                for hh in range(GH):
                    h = g * GH + hh
                    last = pe.matmul(o[32 * hh:32 * hh + 32, :], VN[:, h * VW:(h + 1) * VW], PT[g % 2][:, hh, :],
                                     start=False, stop=True, skip_group_check=True)
                return last

            def tail(g):
                e = g % 2
                do("pe", f"exps_ps_{g}", [f"exps_{g}", before("ot", g, 1)] + (["<x1", "<on"] if g == 0 else []),
                   lambda: exp_transposes(e))
                yield
                do("dve", f"probr_{g}", [f"exps_ps_{g}", "A.countt", before("values", g, 2)],
                   lambda: dve.tensor_tensor(PR[e][:, :], MA[:, 3 * P:4 * P], COUNTT[:, 1, :], ALU.mult))
                do("dve", f"probs_{g}", [],
                   lambda: dve.tensor_tensor(PT[e][:, :, :], TA[:, :].rearrange("p (h q) -> p h q", h=GH),
                                             COUNTT[:, 0, :].unsqueeze(1).to_broadcast([P, GH, P]), ALU.mult))
                yield
                do("pe", f"values_{g}", [f"probs_{g}", "kvnow"], lambda: value_products(g))
                yield
                do("act", f"ot_{g}", [f"values_{g}"] + (["<ot_ps"] if g == 0 else []),
                   lambda: act.activation(OT[:, g, :], MA[:, 0:P], ACT.Copy))

            def head(g):
                e = g % 2
                do("pe", f"scores_{g}", ["kvnow", "A.qt", "A.mask", before("shift", g, 1)], lambda: score_products(g))
                yield
                do("dve", f"max_{g}", [f"scores_{g}"],
                   lambda: dve.tensor_reduce(MAXS[:, e, :].rearrange("p (a h) -> p a h", a=2), scores, AX.X, ALU.max))
                maxs = MAXS[:, e, :].rearrange("p (a h) -> p a h", a=2).unsqueeze(3)
                main = SHIFTED[:, e, 0:GH * P].rearrange("p (a h j) -> p a h j", a=2, h=2)
                rest = SHIFTED[:, e, GH * P:].rearrange("p (a h j) -> p a h j", a=2, h=2)[:, :, :, 0:REST]
                do("dve", f"shiftm_{g}", [f"max_{g}", before("exps", g, 2)],
                   lambda: dve.tensor_tensor(main, scores[:, :, :, 0:P], maxs.to_broadcast([P, 2, 2, P]), ALU.subtract))
                do("dve", f"shift_{g}", [],
                   lambda: dve.tensor_tensor(rest, scores[:, :, :, P:NKV], maxs.to_broadcast([P, 2, 2, REST]),
                                             ALU.subtract))
                yield
                do("act", f"exps_{g}", [f"shift_{g}", before("exps_ps", g, 2)],
                   lambda: act.activation(EXPS[:, e, :], SHIFTED[:, e, :], ACT.Exp))

            yield
            yield from head(0)
            for g in range(1, GROUPS):
                yield from zip_stages(head(g), tail(g - 1))
            yield from tail(GROUPS - 1)
            yield
            do("pe", "ot_ps", ["ot_3", "probs_3"], lambda: transposes(TA[:, :], flat(OT[:, :, :]), GROUPS))
            yield
            attn = TA[:, :].rearrange("p (h w) -> p h w", w=VW)
            do("dve", "rsum", ["ot_ps"], lambda: dve.reciprocal(RSUM[:, :].unsqueeze(2), attn[:, :, DA:DA + 1]))
            do("dve", "on", ["rsum", "<ont_ps"],
               lambda: dve.tensor_tensor(ON[:, :].rearrange("p (h d) -> p h d", d=DA), attn[:, :, 0:DA],
                                         RSUM[:, :].unsqueeze(2).to_broadcast([P, HA, DA]), ALU.mult))
            yield
            do("pe", "ont_ps", ["on"], lambda: transposes(TA[:, :], ON[:, :], KD))
            yield
            do("act", "ont", ["ont_ps", "<y_ps"], lambda: act.activation(flat(ONT[:, :, :]), TA[:, 0:D], ACT.Copy))
            yield

            def y_product():
                for k in range(KD):
                    last = pe.matmul(TA[:, D:2 * D], ONT[:, k, :], WOUT[:, k, :], start=k == 0, stop=k == KD - 1)
                return last

            do("pe", "y_ps", ["ont"], y_product)
            yield
            do("dve", "x1", ["y_ps", "load_xb", "<<C.x1b", "<<C.xm"],
               lambda: dve.tensor_tensor(X1[:, :], TA[:, D:2 * D], XB[:, :], ALU.add))
            yield

        def cols(p):
            return slice(p * P, (p + 1) * P)

        def by_pairs(bank, lhs, rhs, contraction=1):
            for p in range(NP):
                for k in range(contraction):
                    last = pe.matmul(bank[:, cols(p)], lhs(k, p), rhs(k), start=k == 0, stop=k == contraction - 1)
            return last

        def part_c(t, odd, first):
            do = begin_c(t, first)
            X1, X1B, XMT, HQ, HALFE = X1S[odd], X1BS[odd], XMTS[odd], HQS[odd], HALFES[odd]
            CUME, TRIE, ISEXPT, LS3, SG = CUMES[odd], TRIES[odd], ISEXPTS[odd], LS3S[odd], SGS[odd]
            V, VM, K2 = VS[odd], VMS[odd], K2S[odd]
            C0 = F[:, 0, :]
            do("dve", "stats", ["B.x1"], lambda: dve.bn_stats(STATS2[:, :], X1[:, :]))
            do("dve", "meanvar", ["stats"], lambda: dve.bn_aggr(MV2[:, :], STATS2[:, :]), apart=True)
            do("pool", "x1b", ["B.x1", "<<D.out"], lambda: pool.tensor_copy(X1B[:, :], X1[:, :]), apart=True)
            yield
            do("act", "lnvar", ["meanvar"], lambda: act.activation(RSTD2[:, 0:1], MV2[:, 1:2], ACT.Ln, bias=eps))
            do("act", "rstd", ["lnvar"], lambda: act.activation(RSTD2[:, 1:2], RSTD2[:, 0:1], ACT.Exp, scale=-0.5))
            yield
            do("dve", "xm", ["rstd", "<xmt_ps"],
               lambda: dve.tensor_scalar(XM[:, :], X1[:, :], MV2[:, 0:1], RSTD2[:, 1:2], ALU.subtract, ALU.mult))
            yield
            do("pe", "xmt_ps", ["xm", "<k2shift", ">>A.xt"], lambda: transposes(C0, XM[:, :], KD))
            yield
            do("act", "xmt", ["xmt_ps", "<<D.k1_ps"], lambda: act.activation(flat(XMT[:, :, :]), C0[:, 0:D], ACT.Copy))
            yield

            def hidden():
                for k in range(KD):
                    pe.matmul(C0[:, 0:NE], XMT[:, k, :], WE[:, k, :], start=k == 0, stop=k == KD - 1)
                for m in range(2):
                    for k in range(KD):
                        last = pe.matmul(C0[:, (2 + m) * P:(3 + m) * P], WA[:, k, m * P:(m + 1) * P], XMT[:, k, :],
                                         start=k == 0, stop=k == KD - 1)
                return last

            do("pe", "hidden_ps", ["xmt", ">>A.qt"], hidden)
            yield
            do("act", "hid2", ["hidden_ps", "<zg_ps"],
               lambda: act.activation(HID2[:, :], C0[:, 3 * P:4 * P], ACT.Identity, bias=const("onerow")))
            do("act", "hid1", ["<k2_ps", "<hq"], lambda: act.activation(HID1[:, :], C0[:, 2 * P:3 * P], ACT.Copy))
            do("act", "logit", [], lambda: act.activation(LOGIT[:, :], C0[:, 0:NE], ACT.Copy))
            yield
            do("pe", "z0_ps", ["logit"],
               lambda: pe.matmul(C0, HID2[64:96, :], WGB[64:96, :], start=True, stop=True))
            do("dve", "rmax", ["logit"], lambda: dve.tensor_reduce(RT[:, 0:1], LOGIT[:, :], AX.X, ALU.max))
            do("dve", "rnmax", [], lambda: dve.tensor_reduce(RT[:, 1:2], LOGIT[:, :], AX.X, ALU.max, negate=True))
            do("dve", "rvals", ["rmax"],
               lambda: dve.scalar_tensor_tensor(VALS[:, :], LOGIT[:, :], RT[:, 0:1], prio, ALU.is_equal, ALU.mult))
            do("dve", "label", ["rvals"], lambda: dve.tensor_reduce(RT[:, 4:5], VALS[:, :], AX.X, ALU.max))
            yield
            do("act", "zabs0", ["z0_ps", "<ls"], lambda: act.activation(ZABS[:, 0, :], C0, ACT.Abs))
            do("dve", "zmin0", ["zabs0", "<<D.sums_ps"],
               lambda: dve.tensor_scalar(LS3[:, 0, :], C0, 0.0, None, ALU.min))
            do("act", "rexp", ["rnmax"], lambda: act.activation(ELOG[:, :], LOGIT[:, :], ACT.Exp, bias=RT[:, 1:2]))
            yield
            do("pe", "z1_ps", ["zmin0", "zabs0"],
               lambda: pe.matmul(C0, HID2[96:128, :], WGB[96:128, :], start=True, stop=True))
            do("dve", "labb", ["label"], lambda: dve.tensor_copy(LABB[:, :], RT[:, 4:5]))
            do("dve", "isexp", [], lambda: dve.tensor_scalar(ISEXP[:, :], prio, RT[:, 4:5], None, ALU.is_equal))
            do("dve", "rsum", ["rexp"], lambda: dve.tensor_reduce(RT[:, 2:3], ELOG[:, :], AX.X, ALU.add))
            do("dve", "halfe", ["isexp", "<<D.sums_ps"],
               lambda: dve.tensor_tensor(HALFE[:, :, :], const("half").unsqueeze(2).to_broadcast([P, 2, NE]),
                                         ISEXP[:, :].unsqueeze(1).to_broadcast([P, 2, NE]), ALU.mult))
            do("dve", "rweight", ["rsum"], lambda: dve.reciprocal(RT[:, 3:4], RT[:, 2:3]))
            yield
            do("act", "zabs1", ["z1_ps"], lambda: act.activation(ZABS[:, 1, :], C0, ACT.Abs))
            do("dve", "zmin1", ["zabs1"], lambda: dve.tensor_scalar(LS3[:, 1, :], C0, 0.0, None, ALU.min))
            yield
            do("pe", "zg_ps", ["zmin1", "zabs1"],
               lambda: by_pairs(C0, lambda k, p: WGB[0:64, cols(p)], lambda k: HID2[0:64, :]))
            yield
            do("act", "zabs2", ["zg_ps"], lambda: act.activation(ZABS[:, 2, :], C0, ACT.Abs))
            do("act", "zg", ["<sg"], lambda: act.activation(ZG[:, :], C0, ACT.Copy))
            do("dve", "zmin2", ["zg"], lambda: dve.tensor_scalar(LS3[:, 2, :], C0, 0.0, None, ALU.min))
            yield

            def v_product():
                for k in range(KD):
                    last = pe.matmul(C0, XMT[:, k, :], WV[:, k, :], start=k == 0, stop=k == KD - 1)
                return last

            do("pe", "v_ps", ["zmin2", "zg"], v_product)
            do("act", "zexp", ["zabs2"], lambda: act.activation(ZABS[:, :, :], ZABS[:, :, :], ACT.Exp, scale=-1.0))
            yield
            do("act", "v", ["v_ps", "<<D.kvd_ps"], lambda: act.activation(V[:, :], C0, ACT.Copy))
            do("act", "zln", ["zexp"], lambda: act.activation(ZABS[:, :, :], ZABS[:, :, :], ACT.Ln, bias=1.0))
            yield

            def router_rows():
                pe.matmul(C0[:, 0:P], RT[:, 3:4].to_broadcast([P, P]), ident, start=True, stop=True)
                return pe.matmul(C0[:, P:2 * P], LABB[:, 0:1].to_broadcast([P, P]), identb[:, :], start=True, stop=True)

            do("pe", "rows_ps", ["v", "labb", "rweight"], router_rows)
            do("pool", "ls", ["zln", "zmin2"],
               lambda: pool.tensor_tensor(LS3[:, :, :], LS3[:, :, :], ZABS[:, :, :], ALU.subtract))
            yield
            do("dve", "hq", ["rows_ps", "<<D.q2_ps"],
               lambda: dve.tensor_tensor(HQ[0:64, :], HID1[0:64, :], C0[0:64, 0:P], ALU.mult))
            label_row = C0[:, P:2 * P]
            do("dve", "cume", ["<<D.g2_ps"],
               lambda: dve.scalar_tensor_tensor(CUME[:, :], label_row, RT[:, 4:5], cum, ALU.is_equal, ALU.mult))
            do("dve", "trie", ["<<D.at2"],
               lambda: dve.scalar_tensor_tensor(TRIE[:, :], label_row, RT[:, 4:5], tri, ALU.is_equal, ALU.mult))
            do("dve", "isexpt", ["<<D.qm"],
               lambda: dve.tensor_tensor(ISEXPT[:, :, :], label_row.unsqueeze(1).to_broadcast([P, NE, P]),
                                         prio.unsqueeze(2).to_broadcast([P, NE, P]), ALU.is_equal))
            for e in range(NE):
                do("act", "vm" if e == NE - 1 else f"vm{e}", ["v", "isexp", "<<D.kv_ps"],
                   lambda e=e: act.activation(VM[:, :, e, :], V[:, :].rearrange("p (h d) -> p h d", d=DK), ACT.Copy,
                                              scale=ISEXP[:, e:e + 1]))
                if e == 1:
                    yield
            do("act", "sigm", ["ls"], lambda: act.activation(LS3[:, 2, :], LS3[:, 2, :], ACT.Exp))
            yield
            do("pe", "k2_ps", ["isexpt", ">>A.countt"],
               lambda: pe.matmul(C0, HID1[64:128, :], WQKB[64:128, :], start=True, stop=True))
            do("pool", "sg", ["sigm", "zg", "<<D.rmsg"],
               lambda: pool.tensor_tensor(SG[:, :], ZG[:, :], LS3[:, 2, :], ALU.mult))
            yield
            k2p = C0.rearrange("p (h d) -> p h d", d=DK)
            do("dve", "k2max", ["k2_ps"], lambda: dve.tensor_reduce(KS[:, 0, :], k2p, AX.X, ALU.max))
            do("dve", "k2shift", ["k2max", "<<D.k2t_ps"],
               lambda: dve.tensor_tensor(K2[:, :, :], k2p, KS[:, 0, :].unsqueeze(2).to_broadcast([P, H, DK]),
                                         ALU.subtract))
            yield
            do("act", "k2exp", ["k2shift"], lambda: act.activation(K2[:, :, :], K2[:, :, :], ACT.Exp))
            yield
            do("dve", "k2sum", ["k2exp"], lambda: dve.tensor_reduce(KS[:, 1, :], K2[:, :, :], AX.X, ALU.add))
            do("dve", "k2rec", ["k2sum"], lambda: dve.reciprocal(KS[:, 2, :], KS[:, 1, :]))
            do("dve", "k2w", ["k2rec"], lambda: dve.tensor_scalar(KS[:, 3, :], KS[:, 2, :], RT[:, 3:4], None, ALU.mult))
            do("dve", "k2", ["k2w"],
               lambda: dve.tensor_tensor(K2[:, :, :], K2[:, :, :], KS[:, 3, :].unsqueeze(2).to_broadcast([P, H, DK]),
                                         ALU.mult))
            yield

        def part_d(t, odd, first):
            do = begin_d(t, first)
            X1B, XMT, HQ, HALFE = X1BS[odd], XMTS[odd], HQS[odd], HALFES[odd]
            CUME, TRIE, ISEXPT, LS3, SG = CUMES[odd], TRIES[odd], ISEXPTS[odd], LS3S[odd], SGS[odd]
            V, VM, K2, OUT = VS[odd], VMS[odd], K2S[odd], OUTS[odd]
            D0, D1, D2 = (F[:, n, :] for n in (1, 2, 3))
            D12 = F[:, 2:4, :].rearrange("p a (b c) -> p a b c", c=P)
            do("pe", "g1_ps", ["C.ls", "<rmsog"], lambda: by_pairs(D0, lambda k, p: LS3[:, 0, cols(p)], lambda k: cum))
            do("pe", "q1_ps", ["C.xmt", "<out"],
               lambda: by_pairs(D1, lambda k, p: WQ[:, k, cols(p)], lambda k: XMT[:, k, :], KD))
            yield
            do("act", "ep1", ["g1_ps"], lambda: act.activation(EP1[:, :], D0, ACT.Exp))
            do("act", "en1", [], lambda: act.activation(EN1[:, :], D0, ACT.Exp, scale=-1.0))
            do("pe", "k1_ps", ["<rmsln"],
               lambda: by_pairs(D2, lambda k, p: WK[:, k, cols(p)], lambda k: XMT[:, k, :], KD))
            yield
            do("dve", "q1", ["q1_ps", "en1", "<o_ps"],
               lambda: dve.scalar_tensor_tensor(flat(QM[:, NE, :, :]), D1, DK ** -0.5, EP1[:, :], ALU.mult, ALU.mult))
            do("dve", "k1", ["k1_ps"], lambda: dve.tensor_tensor(flat(KG1T[:, :, :]), D2, EN1[:, :], ALU.mult))
            do("pe", "g2_ps", ["C.cume", "en1"],
               lambda: by_pairs(D0, lambda k, p: LS3[:, 1, cols(p)], lambda k: CUME[:, :]))
            yield
            do("act", "en2", ["g2_ps"], lambda: act.activation(EN2[:, :], D0, ACT.Exp, scale=-1.0))
            do("act", "ep2", [], lambda: act.activation(EP2[:, :], D0, ACT.Exp))
            do("pe", "q2_ps", ["q1", "C.hq"],
               lambda: by_pairs(D1, lambda k, p: WQKB[0:64, cols(p)], lambda k: HQ[0:64, :]))
            yield
            do("pe", "k2t_ps", ["C.k2", "ep2"], lambda: transposes(D0, K2[:, :, :].rearrange("p h d -> p (h d)"), NP))
            do("dve", "q2", ["q2_ps", "ep2", "<qm"],
               lambda: dve.scalar_tensor_tensor(flat(QG2[:, :, :]), D1, DK ** -0.5, EP2[:, :], ALU.mult, ALU.mult))
            for e in range(NE):
                do("pool", "qm" if e == NE - 1 else f"qm{e}", ["q2", "<o_ps"],
                   lambda e=e: pool.tensor_tensor(QM[:, e, :, :], QG2[:, :, :],
                                                  ISEXPT[:, e, :].unsqueeze(1).to_broadcast([P, NP, P]), ALU.mult))
            yield
            do("dve", "kg2", ["k2t_ps", "en2"],
               lambda: dve.tensor_tensor(flat(KG2T[:, :, :]), D0, EN2[:, :], ALU.mult))
            yield

            def inner(kt, q):
                for p in range(NP):
                    for par in range(2):
                        r = slice(64 * par, 64 * par + 64)
                        last = pe.matmul((D1, D2)[par][:, cols(p)], kt[r, p, :], q[r, p, :], start=True, stop=True)
                return last

            do("pe", "a1_ps", ["q2", "k1"], lambda: inner(KG1T, QM[:, NE, :, :]))
            do("pe", "k1t_ps", ["kg2"], lambda: transposes(D0, flat(KG1T[:, :, :]), NP))
            yield
            do("dve", "at1", ["a1_ps", "<o_ps"],
               lambda: dve.tensor_tensor(AT1[:, :, :, :].rearrange("p a b c -> p (a b) c"),
                                         D12.rearrange("p a b c -> p (a b) c"),
                                         tri.unsqueeze(1).to_broadcast([P, 2 * NP, P]), ALU.mult))
            do("act", "kg1", ["k1t_ps", "<kvd_ps"], lambda: act.activation(KG1[:, :], D0, ACT.Copy))
            yield
            do("pe", "k2gt_ps", ["kg1"], lambda: transposes(D0, flat(KG2T[:, :, :]), NP))
            do("pe", "a2_ps", ["at1"], lambda: inner(KG2T, QG2[:, :, :]))
            yield
            do("act", "kg2e", ["k2gt_ps", "<kv_ps"], lambda: act.activation(KG2[:, :], D0, ACT.Copy))
            do("dve", "at2", ["a2_ps"],
               lambda: dve.tensor_tensor(AT2[:, :, :, :].rearrange("p a b c -> p (a b) c"),
                                         D12.rearrange("p a b c -> p (a b) c"),
                                         TRIE[:, :].unsqueeze(1).to_broadcast([P, 2 * NP, P]), ALU.mult))
            yield

            def half_sums():
                o = D0[:, 0:2 * NP * ST].rearrange("p (a q e) -> p a q e", a=2, e=ST)
                for p in range(NP):
                    pe.matmul(o[:, :, p, NE], LS3[:, 0, cols(p)], const("half"), start=True, stop=True)
                    last = pe.matmul(o[:, :, p, 0:NE], LS3[:, 1, cols(p)], HALFE[:, :, :], start=True, stop=True)
                return last

            do("pe", "sums_ps", ["kg2e"], half_sums)
            yield
            do("act", "eg", ["sums_ps", "<elast"],
               lambda: act.activation(EG[:, :, :, :].rearrange("p a q e -> p (a q e)"), D0[:, 0:2 * ST * NP], ACT.Exp))
            yield
            do("dve", "dec", ["eg", "<decayd"],
               lambda: dve.scalar_tensor_tensor(flat(DEC[:, :, :]), flat(ELAST[:, :, :]),
                                                CONST[:, bass.ds(_C["keep"][0] + t, 1)],
                                                EG[:, 0, :, :].rearrange("p q e -> p (q e)"), ALU.mult, ALU.mult))
            do("dve", "elast", ["dec"], lambda: dve.tensor_copy(ELAST[:, :, :], EG[:, 1, :, :]))
            do("pool", "decay", ["dec", "<state1"],
               lambda: pool.tensor_tensor(STATE[:, :, :, :], STATE[:, :, :, :],
                                          DEC[:, :, 0:NE].unsqueeze(3).to_broadcast([P, NP, NE, DK]), ALU.mult))
            do("pool", "decayd", ["<stated"],
               lambda: pool.tensor_tensor(STATED[:, :, :], STATED[:, :, :],
                                          DEC[:, :, NE:ST].to_broadcast([P, NP, DK]), ALU.mult))
            yield

            def kv_products():
                for p in range(NP):
                    for par in range(2):
                        h = 2 * p + par
                        o = F[64 * par:64 * par + 64, 2 + p // 2, (p % 2) * NE * DK:(p % 2 + 1) * NE * DK]
                        last = pe.matmul(o, KG2[:, h * DK:(h + 1) * DK], VM[:, h, :, :].rearrange("p e d -> p (e d)"),
                                         start=True, stop=True)
                return last

            def dense_kv_products():
                for p in range(NP):
                    for par in range(2):
                        h = 2 * p + par
                        c = slice(h * DK, (h + 1) * DK)
                        last = pe.matmul(D1[64 * par:64 * par + 64, p * DK:(p + 1) * DK], KG1[:, c], V[:, c],
                                         start=True, stop=True)
                return last

            def inner_outputs():
                for n, at in enumerate((AT1, AT2)):
                    for p in range(NP):
                        for par in range(2):
                            h = 2 * p + par
                            last = pe.matmul(D0[64 * par:64 * par + 64, cols(p)], V[:, h * DK:(h + 1) * DK],
                                             at[:, par, p, :], start=n == 0 and p == 0, stop=False,
                                             skip_group_check=True)
                return last

            def state_outputs():
                for p in range(NP):
                    for e in range(ST):
                        for par in range(2):
                            r = slice(64 * par, 64 * par + 64)
                            state = STATE[r, p, e, :] if e < NE else STATED[r, p, :]
                            last = pe.matmul(D0[r, cols(p)], state, QM[r, e, p, :], start=False,
                                             stop=e == NE, skip_group_check=True)
                return last

            do("pe", "kv_ps", ["at2", "C.vm"], kv_products)
            do("pe", "o_inner", ["eg"], inner_outputs)
            yield
            do("pe", "o_ps", ["decayd", "qm"], state_outputs, apart=True)
            yield
            do("dve", "state1", ["o_ps"],
               lambda: dve.tensor_tensor(STATE[:, :, :, :].rearrange("p (a b) e d -> p a (b e d)", a=2),
                                         STATE[:, :, :, :].rearrange("p (a b) e d -> p a (b e d)", a=2),
                                         F[:, 2:4, :], ALU.add))
            do("act", "sq", ["o_ps"], lambda: act.activation(RMS[:, :], D0, ACT.Square))
            yield
            do("pe", "ms_ps", ["sq", "state1"], lambda: pe.matmul(D2, const("pairs"), RMS[:, :], start=True, stop=True))
            do("pe", "kvd_ps", [], dense_kv_products)
            yield
            do("act", "rmsln", ["ms_ps"], lambda: act.activation(RMS[:, :], D2, ACT.Ln, bias=eps))
            do("act", "rms", ["rmsln"], lambda: act.activation(RMS[:, :], RMS[:, :], ACT.Exp, scale=-0.5))
            do("dve", "stated", ["kvd_ps"],
               lambda: dve.tensor_tensor(flat(STATED[:, :, :]), flat(STATED[:, :, :]), D1[:, 0:NP * DK], ALU.add))
            yield
            do("pool", "rmsg", ["rms", "C.sg"], lambda: pool.tensor_tensor(RMS[:, :], RMS[:, :], SG[:, :], ALU.mult))
            yield
            do("dve", "rmsog", ["rmsg"],
               lambda: dve.tensor_tensor(flat(OG[:, :, :]), D0, RMS[:, :], ALU.mult))
            yield

            def out_product():
                for p in range(NP):
                    last = pe.matmul(D1[:, D:2 * D], OG[:, p, :], WO[:, p, :], start=p == 0, stop=p == NP - 1)
                return last

            do("pe", "y_ps", ["rmsog"], out_product)
            yield
            do("dve", "out", ["y_ps", "C.x1b", "<store"],
               lambda: dve.tensor_tensor(OUT[:, :], D1[:, D:2 * D], X1B[:, :], ALU.add))
            do("sp", "store", ["out"], lambda: sp.dma_start(out[bass.ts(t, P), :], OUT[:, :]), dma=True)
            yield

        parts = (part_a, part_b, part_c, part_d)
        lag = len(parts) - 1

        def iteration(i, odd, first):
            running = {}
            for n, part in enumerate(parts):
                if first - n >= 0 and not (isinstance(i, int) and i - n >= TILES):
                    running["ABCD"[n]] = part(i - n, (odd + n) % 2, first - n)
            for name in order:
                if name in running:
                    next(running[name], None)
            assert all(next(g, "end") == "end" for g in running.values())

        length = {name: sum(1 for _ in part(0, 0, 0)) + 1 for name, part in zip("ABCD", parts)}
        turns = TURNS
        assert all(turns.count(n) == length[n] for n in "AC"), length
        slots = [(k / len(turns), name) for k, name in enumerate(turns)]
        slots += [(k / length[name], name) for name in "BD" for k in range(length[name])]
        order = [name for _, name in sorted(slots)]
        steps.dry = False
        start = lag + 1
        for i in range(start):
            iteration(i, i % 2, i)
        with nc.Fori(start // 2, TILES // 2) as pair:
            for odd in range(2):
                iteration(pair * 2 + odd, odd, start + odd)
        for i in range(TILES, TILES + lag):
            iteration(i, i % 2, i)
        steps.wait("D", "sp", "store")


def zip_stages(*parts):
    live = list(parts)
    while live:
        for g in list(live):
            if next(g, "end") == "end":
                live.remove(g)
        yield


def kernel(**inputs):
    import concourse.bacc as bacc
    from concourse.bass_utils import run_bass_kernel_spmd

    def a(name):
        return np.asarray(inputs[name])

    def blocks(w):
        return np.ascontiguousarray(w.reshape(-1, P, w.shape[1]).transpose(1, 0, 2))

    f = "L0_ffn_"
    pad = np.zeros((D, 16), np.float32)
    gap = np.zeros((15, HD), np.float32)
    arrays = {
        "x": a("x").reshape(B * L, D),
        "idx": a("itok_BxSx64_0_2047").reshape(B * L, PICKS),
        "ctxT": blocks(a("ctx_1024").reshape(B * NKV, D).T),
        "consts": constants(),
        "w_q": blocks(a("L0_xattn_W_q").T),
        "w_down": blocks(a("L0_xattn_W_kv_down").T),
        "w_up": a("L0_xattn_W_kv_up").T,
        "w_out": blocks(a("L0_xattn_W_out").T),
        "wa": blocks(np.concatenate([a(f + "Wqa"), a(f + "Wka"), a(f + "Wga"), a(f + "Wg1a"), pad, a(f + "Wg2a"), pad], 1)),
        "we": blocks(a(f + "We")),
        "wq": blocks(a(f + "Wq")),
        "wk": blocks(a(f + "Wk")),
        "wv": blocks(a(f + "Wv")),
        "wqk_b": np.concatenate([a(f + "Wqb"), a(f + "Wkb")]),
        "wg_b": np.concatenate([a(f + "Wgb"), a(f + "Wg1b"), a(f + "bg1")[None], gap, a(f + "Wg2b"), a(f + "bg2")[None], gap]),
        "wo": blocks(a(f + "Wo")),
        "norm_w": np.concatenate([a(f + "norm_w"), a(f + "norm_w")])[:, None],
    }
    nc = bacc.Bacc("TRN2", target_bir_lowering=False, num_devices=1)
    args, fed = [], {}
    for name, v in arrays.items():
        v = np.ascontiguousarray(v)
        fed[name + "_dram"] = v
        args.append(nc.dram_tensor(name + "_dram", v.shape, mybir.dt.from_np(v.dtype), kind="ExternalInput").ap())
    out = nc.dram_tensor("out_dram", (B * L, D), mybir.dt.float32, kind="ExternalOutput").ap()
    program(nc, *args, out)
    r = run_bass_kernel_spmd(nc, [fed], core_ids=[0])
    return r.results[0]["out_dram"].reshape(B, L, D)
```

```python
import numpy as np
import concourse.bass as bass
from concourse import mybir
from contextlib import ExitStack

P = 128
B, L, D = 4, 1024, 256
TILES = B * L // P
TPB = L // P
KD = D // P
NKV, PICKS = 154, 64
HA, DA = 16, 16
REST = NKV - P
RPAD, NPAD = 32, 160
BASES, DIGIT = 52, 7
GROUPS, GH = 4, 4
VW = 32
VALW = 2 * HA * VW
HB = HA // KD
PARTS = 3
Q_SLABS = (0, 1, 2, 0, 1, 2, 0, 1)
K_SLABS = (0, 0, 0, 1, 1, 1, 2, 2)
GR = 17
Z_SLABS = (0, 1, 2, 0, 1, 2, 0)
W_SLABS = (0, 0, 0, 1, 1, 1, 2)
H, DK = 8, 64
HD = H * DK
NP = HD // P
NE = 4
EH = NE // 2
NS = H * EH
NORMALIZER = 16.0
EPS = 1e-5
MASKED = -1e30

_C = {}
_n = 0
for _name, _w in (("ident", P), ("cum", P), ("tri", P), ("half", 2), ("prio", NE), ("prio_half", EH), ("onerow", 1), ("eps", 1), ("pairs", P),
                  ("bases", BASES), ("quarter", GH), ("keep", TILES)):
    _C[_name] = (_n, _n + _w)
    _n += _w
NCONST = _n


def constants():
    c = np.zeros((P, NCONST), np.float32)
    r = np.arange(P)
    s, t = r[:, None], r[None, :]
    mid = P // 2

    def put(name, v):
        c[:, _C[name][0]:_C[name][1]] = v

    put("ident", s == t)
    put("cum", (((s >= mid) & (s <= t)) * 1.0 - ((s < mid) & (s > t)) * 1.0) / NORMALIZER)
    put("tri", s <= t)
    put("half", np.stack([r < mid, r >= mid], 1) / NORMALIZER)
    put("prio", np.arange(NE, 0, -1)[None, :])
    put("prio_half", NE - 2 * np.arange(EH)[None, :] - (s >= DK))
    put("onerow", ((r == 80) | (r == 112))[:, None])
    put("eps", EPS)
    put("pairs", (s // DK == t // DK) / DK)
    put("bases", np.arange(BASES)[None, :])
    put("quarter", (r // RPAD)[:, None] == np.arange(GH)[None, :])
    put("keep", (np.arange(TILES) % TPB != 0)[None, :])
    return c


ORDER = """
A3 B1 A1 C1 D1 B1 A1 D1 A2 B2 A1 D1 A3 D1 A2 D4 C1 B3 A2 D1 A3 B1 A1 B1 C2 B1 C1 B1 D1 C1 D1 B2 A2 D1 A1 B1 C1
B1 C1 D1 B3 A4 B2 C1 A2 C1 D1 C4 A1 C1 D3 A1 C1 D2 B1 C2 D3 B2 C1 B1 C2 B1 C2 D1 C7 A1 C2 D1 B2 A2 B1 D2 C1 B1
C2 D2 B2 D1 B1 D1 B1 C1 A1 C2 B1 C1 B1 D3 C2 D3 C2 B1 A1 D3 C1 B2 C1 B2 A1 C1 D1 B2 C1 A1 C1 A1 C1 B1 C8 D1 A2
C1 A1 D4 A1 B2 A1 D1 B1 D1 B1 C1 B1 C1 D1 C1 D3 C2 B2 D1 B1 D1 C2 B1 D1 C3
"""


class Steps:

    def __init__(self, nc, ctx):
        self.nc, self.ctx = nc, ctx
        self.engines = {"pe": nc.tensor, "dve": nc.vector, "act": nc.scalar, "pool": nc.gpsimd, "sp": nc.sync}
        self.gate = ctx.enter_context(nc.semaphore("gate"))
        self.sems, self.total, self.number = {}, {}, {}
        self.dry = True
        self.tile = {}
        self.waited = {}

    def begin(self, part, tile, first):
        self.tile[part] = tile, first
        for key in [k for k in self.waited if k[0] == part]:
            del self.waited[key]

    def do(self, part, engine, name, after, issue, dma=False, apart=False):
        lane = (part, name if dma else engine)
        if self.dry:
            self.total[lane] = self.total.get(lane, 0) + 1
            if lane not in self.sems:
                self.sems[lane] = self.ctx.enter_context(self.nc.semaphore("done_" + "_".join(lane)))
            self.number[f"{part}.{name}"] = (lane, self.total[lane], 16 if dma else 1)
            return
        for a in after:
            self.wait(part, engine, a)
        if apart and after:
            self.engines[engine].sem_inc(self.gate, 1)
        issue().then_inc(self.sems[lane], 16 if dma else 1)

    def wait(self, part, engine, what):
        name = what.lstrip("<>")
        back = what.count("<") - what.count(">")
        if "." not in name:
            name = f"{part}.{name}"
        lane, number, unit = self.number[name]
        tile, first = self.tile[part]
        if first < back or isinstance(tile, int) and tile - back >= TILES:
            return
        number -= self.total[lane] * back
        if number <= self.waited.get((part, engine, lane), -10 ** 9):
            return
        self.waited[(part, engine, lane)] = number
        self.engines[engine].wait_ge(self.sems[lane], (tile * self.total[lane] + number) * unit)


def program(nc, x, idx, ctxT, consts, w_q, w_down, w_up, w_out, wa, we, wq, wk, wv, wqk_b, wg_b, wo, norm_w, out):
    f32, bf16, i32 = mybir.dt.float32, mybir.dt.bfloat16, mybir.dt.int32
    ALU, ACT, AX = mybir.AluOpType, mybir.ActivationFunctionType, mybir.AxisListType
    pe, dve, act, pool, sp = nc.tensor, nc.vector, nc.scalar, nc.gpsimd, nc.sync

    with ExitStack() as ctx:
        def sb(name, shape, dt=f32):
            return ctx.enter_context(nc.sbuf_tensor(name, shape, dt))

        def ps(name, shape):
            return ctx.enter_context(nc.psum_tensor(name, shape, f32))

        def sem(name):
            return ctx.enter_context(nc.semaphore(name))

        CONST = sb("CONST", [P, NCONST])

        def const(name):
            return CONST[:, _C[name][0]:_C[name][1]]

        ident, cum, tri = const("ident"), const("cum"), const("tri")
        prio, eps = const("prio"), const("eps")
        WQ_A = sb("WQ_A", [P, KD, D])
        WOUT = sb("WOUT", [P, KD, D])
        WA = sb("WA", [P, KD, 256])
        WE = sb("WE", [P, KD, NE])
        WQ = sb("WQ", [P, KD, HD])
        WK = sb("WK", [P, KD, HD])
        WV = sb("WV", [P, KD, HD])
        WQKB = sb("WQKB", [P, HD])
        WGB = sb("WGB", [P, HD])
        ZW = sb("ZW", [P, 2, HD], bf16)
        WO = sb("WO", [P, NP, D])
        NORMW = sb("NORMW", [P, 1])
        identb = sb("identb", [P, P], bf16)
        BASETAB = sb("BASETAB", [P, BASES, PICKS], bf16)

        SA = ps("SA", [P, 2, 512])
        TA = ps("TA", [P, 512])
        MA = ps("MA", [P, 512])
        F = ps("F", [P, 4, 512])

        s_w = sem("s_w")
        s_pe0 = sem("s_pe0")
        s_dve0 = sem("s_dve0")
        s_act0 = sem("s_act0")
        s_kv = sem("s_kv")
        s_split = sem("s_split")
        s_gate = sem("s_gate")
        steps = Steps(nc, ctx)

        brief = ExitStack()

        def brief_sb(name, shape):
            return brief.enter_context(nc.sbuf_tensor(name, shape, f32))

        WDOWN = brief_sb("WDOWN", [P, KD, P])
        WUP = brief_sb("WUP", [P, 2 * D])
        CTXT = brief_sb("CTXT", [P, KD, B * NKV])
        CT = brief_sb("CT", [P, B, NKV])
        CREST = brief_sb("CREST", [P, B, GH, RPAD])
        KT = brief_sb("KT", [P, B, KD, NKV])
        WREST = brief_sb("WREST", [P, HD])
        WPARTS = brief.enter_context(nc.sbuf_tensor("WPARTS", [P, PARTS, HD], bf16))
        KPARTS = brief.enter_context(nc.sbuf_tensor("KPARTS", [P, PARTS, B, KD, NKV], bf16))
        VALL = brief_sb("VALL", [P, B, HA, VW])
        VRALL = brief_sb("VRALL", [P, B, GROUPS * GH * VW])
        k_dram = nc.dram_tensor("k_dram", (B * P, HA * NKV), bf16).ap()
        v_dram = nc.dram_tensor("v_dram", (B * P, VALW), f32).ap()
        w_dram = nc.dram_tensor("w_dram", (PARTS * GR, 2 * HD), bf16).ap()
        z_dram = nc.dram_tensor("z_dram", (PARTS * GR, 2 * P), bf16).ap()
        q_dram = nc.dram_tensor("q_dram", (PARTS * P, KD * P), bf16).ap()
        loads = [(CONST[:, :], consts), (CTXT[:, :, :], ctxT), (WDOWN[:, :, :], w_down), (WUP[:, :], w_up),
                 (WQ_A[:, :, :], w_q), (WOUT[:, :, :], w_out), (WA[:, :, :], wa), (WE[:, :, :], we),
                 (WQ[:, :, :], wq), (WK[:, :, :], wk), (WV[:, :, :], wv), (WQKB[:, :], wqk_b), (WGB[:, :], wg_b),
                 (WO[:, :, :], wo), (NORMW[:, :], norm_w)]
        for n, (dst, src) in enumerate(loads):
            (sp if n % 2 == 0 else act).dma_start(dst, src).then_inc(s_w, 16)
        act.preload_act_table_set("natural_log_exp_and_others")
        pool.memset(VALL[:, :, :, :], 0.0)
        pool.memset(VRALL[:, :, :], 0.0)
        pool.memset(CREST[:, :, :, :], 0.0).then_inc(s_act0, 1)
        for e in (pe, dve, act, pool):
            e.wait_ge(s_w, 16 * len(loads))
        for n in range(PARTS):
            rest = WGB if n == 0 else WREST
            pool.wait_ge(s_gate, 2 * n)
            pool.tensor_copy(WPARTS[:, n, :], rest[:, :]).then_inc(s_gate, 1)
            if n < PARTS - 1:
                pool.wait_ge(s_gate, 2 * n + 1)
                pool.tensor_tensor(WREST[:, :], rest[:, :], WPARTS[:, n, :], ALU.subtract).then_inc(s_gate, 1)
        half = 2 * NKV
        for c in range(2):
            for k in range(KD):
                last = pe.matmul(F[:, c, 0:half], WDOWN[:, k, :], CTXT[:, k, c * half:(c + 1) * half],
                                 start=k == 0, stop=k == KD - 1)
        last.then_inc(s_pe0, 1)
        dve.wait_ge(s_pe0, 1)
        CTf = CT[:, :, :].rearrange("p b j -> p (b j)")
        for c in range(2):
            last = dve.tensor_copy(CTf[:, c * half:(c + 1) * half], F[:, c, 0:half])
        last.then_inc(s_dve0, 1)
        dve.wait_ge(s_dve0, 1)
        dve.wait_ge(s_act0, 1)
        for hh in range(GH):
            last = dve.tensor_copy(CREST[:, :, hh, 0:REST], CT[:, :, P:NKV])
        last.then_inc(s_dve0, 1)
        pe.wait_ge(s_dve0, 1)
        for blk in range(KD):
            for c in range(2):
                bank = SA[:, c, 0:half] if blk == 0 else (TA, MA)[c][:, 0:half]
                last = pe.matmul(bank, WUP[:, blk * P:(blk + 1) * P], CTf[:, c * half:(c + 1) * half],
                                 start=True, stop=True)
        last.then_inc(s_pe0, 1)
        dve.wait_ge(s_pe0, 2)
        for blk in range(KD):
            for c in range(2):
                bank = SA[:, c, 0:half] if blk == 0 else (TA, MA)[c][:, 0:half]
                last = dve.tensor_scalar(KT[:, 2 * c:2 * c + 2, blk, :], bank.rearrange("p (b j) -> p b j", b=2),
                                         DA ** -0.5, None, ALU.mult)
        last.then_inc(s_split, 1)
        keys = KT[:, :, :, :].rearrange("p b k j -> p (b k j)")
        for n in range(PARTS):
            part = KPARTS[:, n, :, :, :].rearrange("p b k j -> p (b k j)")
            dve.wait_ge(s_split, 2 * n + 1)
            dve.tensor_copy(part, keys).then_inc(s_split, 1)
            if n < PARTS - 1:
                dve.wait_ge(s_split, 2 * n + 2)
                dve.tensor_tensor(keys, keys, part, ALU.subtract).then_inc(s_split, 1)
        pe.wait_ge(s_dve0, 2)
        for b in range(B):
            pe.matmul(F[:, b, 0:D], CT[:, b, 0:P], WUP[:, D:2 * D], start=True, stop=True)
            last = pe.matmul(F[:, b, D:2 * D], CREST[:, b, :, :].rearrange("p h j -> p (h j)"), WUP[:, D:2 * D], start=True, stop=True)
        last.then_inc(s_pe0, 1)
        dve.wait_ge(s_pe0, 3)
        dve.memset(VALL[:, :, :, DA:DA + 1], 1.0)
        VR5 = VRALL[:, :, :].rearrange("p b (g h w) -> p b g h w", g=GROUPS, h=GH)
        for b in range(B):
            dve.tensor_copy(VALL[:, b, :, 0:DA], F[:, b, 0:D].rearrange("p (h d) -> p h d", d=DA))
        rest = F[:, :, D:2 * D].rearrange("p b (g h d) -> p b g h d", g=GROUPS, h=GH)
        for hh in range(GH):
            quarter = const("quarter")[:, hh:hh + 1]
            dve.tensor_scalar(VR5[:, :, :, hh, 0:DA], rest[:, :, :, hh, :], quarter, None, ALU.mult)
            last = dve.tensor_copy(VR5[:, :, :, hh, DA], quarter.unsqueeze(1).to_broadcast([P, B, GROUPS]))
        last.then_inc(s_dve0, 1)
        for p in range(NP):
            dve.tensor_scalar(WO[:, p, :], WO[:, p, :], NORMW[:, 0:1], None, ALU.mult)
        dve.tensor_copy(identb[:, :], ident)
        dve.tensor_copy(BASETAB[:, :, :], const("bases").unsqueeze(2).to_broadcast([P, BASES, PICKS]))
        sp.wait_ge(s_gate, 2 * PARTS - 1)
        w_rows = w_dram.rearrange("(n r) (g w) -> r g n w", n=PARTS, g=2)
        for g in range(2):
            first = P // 2 + 32 * g
            sp.dma_start(w_rows[:, g], WPARTS[first:first + GR, :, :]).then_inc(s_kv, 16)
        sp.wait_ge(s_kv, 32)
        for n, part in enumerate(W_SLABS):
            sp.dma_start(ZW[n * GR:(n + 1) * GR, :, :].rearrange("r g w -> r (g w)"),
                         w_dram[part * GR:(part + 1) * GR, :]).then_inc(s_kv, 16)
        sp.wait_ge(s_split, 2 * PARTS)
        k_rows = k_dram.rearrange("(b s d) (h w) -> s (d h) b w", b=B, d=DA, h=HB)
        for n, part in enumerate(K_SLABS):
            sp.dma_start(k_rows[n], KPARTS[:, part, :, :, :].rearrange("p b k j -> p b (k j)")).then_inc(s_kv, 16)
        sp.wait_ge(s_dve0, 3)
        v_rows = v_dram.rearrange("(b p) w -> p b w", p=P)
        for c0, src in ((0, VALL[:, :, :, :].rearrange("p b h w -> p b (h w)")), (HA * VW, VRALL[:, :, :])):
            sp.dma_start(v_rows[:, :, c0:c0 + src.shape[2]], src).then_inc(s_kv, 16)
        sp.wait_ge(s_kv, 16 * (2 + len(W_SLABS) + 2 + len(K_SLABS)))
        nc.all_engine_barrier()
        brief.close()

        def two(name, shape, dt=f32):
            return [sb(f"{name}{i}", shape, dt) for i in range(2)]

        KNOW = two("KNOW", [P, HA, NKV], bf16)
        VNOW = two("VNOW", [P, VALW])

        XA = sb("XA", [P, D])
        IDX = sb("IDX", [P, PICKS], i32)
        IW = [sb(f"IW{i}", [P, PICKS]) for i in range(6)]
        BASE = sb("BASE", [P, PICKS], bf16)
        WEIGHT = sb("WEIGHT", [P, PICKS], bf16)
        HOT = sb("HOT", [P, BASES, PICKS], bf16)
        PACKED = sb("PACKED", [P, BASES], i32)
        COUNTI = sb("COUNTI", [P, NPAD], i32)
        COUNT = sb("COUNT", [P, NPAD])
        COUNTR = sb("COUNTR", [P, GH, RPAD])
        STATS = sb("STATS", [P, 6])
        MV = sb("MV", [P, 2])
        RSTD = sb("RSTD", [P, 2])
        XN = sb("XN", [P, D])
        XNT = sb("XNT", [P, KD, P])
        MASKS = two("MASK", [P, NKV], bf16)
        COUNTTS = two("COUNTT", [P, 2, P])
        QT = sb("QT", [P, KD, P])
        QREST = sb("QREST", [P, KD, P])
        QPARTS = sb("QPARTS", [P, PARTS, KD, P], bf16)
        QSS = two("QS", [P, HA, P], bf16)

        XB = sb("XB", [P, D])
        MAXS = sb("MAXS", [P, 2, GH])
        EXPS = sb("EXPS", [P, 2, GH, NPAD])
        PT = two("PT", [P, GH, P])
        PR = two("PR", [P, P])
        OT = sb("OT", [P, GROUPS, P])
        RSUM = sb("RSUM", [P, HA])
        ON = sb("ON", [P, D])
        ONT = sb("ONT", [P, KD, P])
        X1S = two("X1", [P, D])

        STATS2 = sb("STATS2", [P, 6])
        MV2 = sb("MV2", [P, 2])
        RSTD2 = sb("RSTD2", [P, 2])
        XM = sb("XM", [P, D])
        HID1 = sb("HID1", [P, P])
        HID2 = sb("HID2", [P, P])
        LOGIT = sb("LOGIT", [P, NE])
        RT = sb("RT", [P, 8])
        VALS = sb("VALS", [P, NE])
        ELOG = sb("ELOG", [P, NE])
        ISEXP = sb("ISEXP", [P, NE])
        LABB = sb("LABB", [P, 1], bf16)
        ZABS = sb("ZABS", [P, 3, HD])
        ZPARTS = sb("ZPARTS", [P, PARTS, P], bf16)
        ZREST = sb("ZREST", [P, P])
        ZS = sb("ZS", [P, 2, P], bf16)
        KS = sb("KS", [P, 4, H])
        X1BS = two("X1B", [P, D])
        XMTS = two("XMT", [P, KD, P])
        HQS = two("HQ", [P, P])
        HALFES = two("HALFE", [P, 2, 2, EH])
        CUMES = two("CUME", [P, P])
        TRIES = two("TRIE", [P, P])
        ISEXPTS = two("ISEXPT", [P, EH, P])
        LS3S = two("LS3_", [P, 3, HD])
        SGS = two("SG", [P, HD])
        VS = two("V", [P, HD])
        VMS = two("VM", [P, H, 2, EH, DK])
        K2S = two("K2_", [P, H, DK])

        EP = sb("EP", [P, HD])
        EN1 = sb("EN1", [P, HD])
        EN2 = sb("EN2", [P, HD])
        KG1T = sb("KG1T", [P, NP, P])
        KG2T = sb("KG2T", [P, NP, P])
        QG2 = sb("QG2", [P, NP, P])
        Q1 = sb("Q1", [P, NP, P])
        QD = sb("QD", [P, 2, NP, P])
        QM = sb("QM", [P, EH, 2, NP, P])
        KG1 = sb("KG1", [P, HD])
        KG2 = sb("KG2", [P, HD])
        AT1 = sb("AT1", [P, 2, NP, P])
        AT2 = sb("AT2", [P, 2, NP, P])
        EG = sb("EG", [P, 2, NS + NP])
        ELAST = sb("ELAST", [P, NS + NP])
        DEC = sb("DEC", [P, NS + NP])
        STATE = sb("STATE", [P, H, EH, DK])
        STATED = sb("STATED", [P, NP, DK])
        RMS = sb("RMS", [P, HD])
        OG = sb("OG", [P, NP, P])
        OUT = sb("OUT", [P, D])

        pool.memset(COUNTI[:, :], 0)
        pool.memset(EXPS[:, :, :, :], 0.0)
        pool.memset(STATE[:, :, :, :], 0.0)
        pool.memset(STATED[:, :, :], 0.0)
        pool.memset(ELAST[:, :], 0.0)
        nc.all_engine_barrier()

        def transposes(bank, src, n):
            for k in range(n):
                last = pe.transpose(bank[:, k * P:(k + 1) * P], src[:, k * P:(k + 1) * P], ident)
            return last

        def flat(a):
            return a.rearrange("p a b -> p (a b)")

        def starter(part):
            def begin(t, first):
                steps.begin(part, t, first)

                def do(engine, name, after, issue, dma=False, apart=False):
                    steps.do(part, engine, name, after, issue, dma, apart)
                return do
            return begin

        begin_a, begin_b, begin_c, begin_d = (starter(x) for x in "ABCD")
        spare = [F[:, 0, i * P:(i + 1) * P] for i in range(2)]
        spares = F[:, 0, 0:D].rearrange("p (k t) -> p k t", k=KD)

        def part_a(t, odd, first):
            do = begin_a(t, first)
            MASK, COUNTT, QS = MASKS[odd], COUNTTS[odd], QSS[odd]
            rows = bass.ts(t, P)
            yield do("sp", "load_idx", ["<idx_float"], lambda: sp.dma_start(IDX[:, :], idx[rows, :]), dma=True)
            yield do("sp", "load_xa", ["<xn"], lambda: sp.dma_start(XA[:, :], x[rows, :]), dma=True)
            yield do("sp", "know", ["<<B.values_3"],
               lambda: sp.dma_start(KNOW[odd][:, :, :].rearrange("p h j -> p (h j)"), k_dram[bass.ts(t // TPB, P), :]),
               dma=True)
            yield do("sp", "vnow", [], lambda: sp.dma_start(VNOW[odd][:, :], v_dram[bass.ts(t // TPB, P), :]), dma=True)
            yield do("pool", "idx_float", ["load_idx", "<idx_clamp"], lambda: pool.tensor_copy(IW[1][:, :], IDX[:, :]),
               apart=True)
            yield do("pool", "idx_wrap1", ["idx_float"],
               lambda: pool.tensor_scalar(IW[0][:, :], IW[1][:, :], 0.0, float(NKV), ALU.is_lt, ALU.mult), apart=True)
            yield do("pool", "idx_wrap2", ["idx_wrap1"],
               lambda: pool.tensor_tensor(IW[1][:, :], IW[1][:, :], IW[0][:, :], ALU.add))
            yield do("pool", "idx_clamp", ["idx_wrap2", "<weight"],
               lambda: pool.tensor_scalar(IW[2][:, :], IW[1][:, :], float(NKV - 1), 0.0, ALU.min, ALU.max), apart=True)
            yield do("pool", "digit1", ["idx_clamp"],
               lambda: pool.tensor_scalar(IW[3][:, :], IW[2][:, :], float(BASES), None, ALU.is_ge), apart=True)
            yield do("pool", "digit2", [],
               lambda: pool.tensor_scalar(IW[4][:, :], IW[2][:, :], float(2 * BASES), None, ALU.is_ge))
            yield do("dve", "stats", ["load_xa"], lambda: dve.bn_stats(STATS[:, :], XA[:, :]))
            yield do("dve", "meanvar", ["stats"], lambda: dve.bn_aggr(MV[:, :], STATS[:, :]), apart=True)
            yield do("act", "lnvar", ["meanvar"], lambda: act.activation(RSTD[:, 0:1], MV[:, 1:2], ACT.Ln, bias=eps))
            yield do("act", "rstd", ["lnvar"], lambda: act.activation(RSTD[:, 1:2], RSTD[:, 0:1], ACT.Exp, scale=-0.5))
            yield do("dve", "digits", ["digit2"],
               lambda: dve.tensor_tensor(IW[5][:, :], IW[3][:, :], IW[4][:, :], ALU.add))
            yield do("dve", "weight1", ["digits"],
               lambda: dve.tensor_scalar(IW[3][:, :], IW[3][:, :], float(2 ** DIGIT - 1), 1.0, ALU.mult, ALU.add))
            yield do("dve", "base", [],
               lambda: dve.scalar_tensor_tensor(BASE[:, :], IW[5][:, :], float(-BASES), IW[2][:, :], ALU.mult, ALU.add))
            yield do("dve", "weight", ["weight1"],
               lambda: dve.scalar_tensor_tensor(WEIGHT[:, :], IW[4][:, :], float(4 ** DIGIT - 2 ** DIGIT), IW[3][:, :],
                                                ALU.mult, ALU.add))
            yield do("dve", "xn", ["rstd", "<xt_ps"],
               lambda: dve.tensor_scalar(XN[:, :], XA[:, :], MV[:, 0:1], RSTD[:, 1:2], ALU.subtract, ALU.mult))
            yield do("dve", "hot", ["weight"],
               lambda: dve.tensor_tensor(HOT[:, :, :], BASE[:, :].unsqueeze(1).to_broadcast([P, BASES, PICKS]),
                                         BASETAB[:, :, :], ALU.is_equal))

            def xt_transposes():
                pe.transpose(spare[0], XN[:, 0:P], ident)
                return pe.transpose(spare[1], XN[:, P:2 * P], ident)

            yield do("pe", "xt_ps", ["xn", "<countt", "<<<C.k2shift"], xt_transposes)
            yield do("act", "xt", ["xt_ps", "<q_ps"], lambda: act.activation(XNT[:, :, :], spares, ACT.Copy))

            def q_product():
                for m in range(KD):
                    for k in range(KD):
                        last = pe.matmul(spare[m], WQ_A[:, k, m * P:(m + 1) * P], XNT[:, k, :],
                                         start=k == 0, stop=k == KD - 1)
                return last

            yield do("pe", "q_ps", ["xt", "<<C.xmt"], q_product)
            yield do("dve", "hotw", ["hot"],
               lambda: dve.tensor_tensor(HOT[:, :, :], HOT[:, :, :],
                                         WEIGHT[:, :].unsqueeze(1).to_broadcast([P, BASES, PICKS]), ALU.mult))
            yield do("act", "qt", ["q_ps", "<qrest"], lambda: act.activation(QT[:, :, :], spares, ACT.Copy))
            yield do("act", "qpart0", ["qt", "<qstore"], lambda: act.activation(QPARTS[:, 0, :, :], QT[:, :, :], ACT.Copy))
            yield do("pool", "qrest", ["qpart0", "<qpart2"],
               lambda: pool.tensor_tensor(QREST[:, :, :], QT[:, :, :], QPARTS[:, 0, :, :], ALU.subtract))
            yield do("act", "qpart1", ["qrest"], lambda: act.activation(QPARTS[:, 1, :, :], QREST[:, :, :], ACT.Copy))
            yield do("pool", "qpart2", ["qpart1", "<qslabs0", "<qslabs1", "<qslabs2", "<<B.scores_3"],
               lambda: pool.tensor_tensor(QPARTS[:, 2, :, :], QREST[:, :, :], QPARTS[:, 1, :, :], ALU.subtract), apart=True)
            yield do("sp", "qstore", ["qpart2"],
               lambda: sp.dma_start(q_dram.rearrange("(n p) w -> p n w", n=PARTS),
                                    QPARTS[:, :, :, :].rearrange("p n k t -> p n (k t)")), dma=True)
            q_rows = q_dram.rearrange("(n d h) w -> (n d) (h w)", d=DA, h=HB)
            for n in range(PARTS):
                slabs = slice(n * PARTS, min(n * PARTS + PARTS, len(Q_SLABS)))
                size = DA * (slabs.stop - slabs.start)
                yield do("sp", f"qslabs{n}", ["qstore"],
                   lambda: sp.dma_start(QS[slabs.start * DA:slabs.stop * DA, :, :].rearrange("p h t -> p (h t)"),
                                        q_rows[0:size, :]), dma=True)

            def pack(r):
                with nc.allow_low_precision(reason="whole numbers below 2**24, summed in float32"):
                    return dve.tensor_reduce(PACKED[:, r], HOT[:, r, :], AX.X, ALU.add)

            yield do("dve", "packed0", ["hotw"], lambda: pack(slice(0, BASES // 2)))
            yield do("dve", "packed", [], lambda: pack(slice(BASES // 2, BASES)))
            low = 2 ** DIGIT - 1
            yield do("dve", "cut0", ["packed"], lambda: dve.tensor_scalar(
                COUNTI[:, 0:BASES], PACKED[:, :], low, None, ALU.bitwise_and))
            for d in range(1, 3):
                yield do("dve", f"cut{d}", [], lambda d=d: dve.tensor_scalar(
                    COUNTI[:, d * BASES:(d + 1) * BASES], PACKED[:, :], d * DIGIT, low,
                    ALU.logical_shift_right, ALU.bitwise_and))
            yield do("dve", "count", ["cut2", "<count_ps"], lambda: dve.tensor_copy(COUNT[:, :], COUNTI[:, :]))
            yield do("dve", "countr", [],
               lambda: dve.tensor_copy(COUNTR[:, :, :], COUNTI[:, P:NPAD].unsqueeze(1).to_broadcast([P, GH, RPAD])))
            yield do("dve", "mask", ["count", "<<B.scores_3"],
               lambda: dve.tensor_scalar(MASK[:, :], COUNT[:, 0:NKV], 0.0, MASKED, ALU.is_equal, ALU.mult))

            def count_transposes():
                pe.transpose(spare[0], COUNT[:, 0:P], ident)
                return pe.transpose(spare[1], COUNTR[:, :, :].rearrange("p h j -> p (h j)"), ident)

            yield do("pe", "count_ps", ["countr", "qt", "<<C.isexpt"], count_transposes)
            yield do("act", "countt", ["count_ps", "<<B.probs_3"], lambda: act.activation(COUNTT[:, :, :], spares, ACT.Copy))

        def part_b(t, odd, first):
            do = begin_b(t, first)
            MASK, COUNTT, QS, X1 = MASKS[odd], COUNTTS[odd], QSS[odd], X1S[odd]
            KN, V1 = KNOW[odd], VNOW[odd]
            VN, VR = V1[:, 0:HA * VW], V1[:, HA * VW:VALW]
            yield do("sp", "load_xb", ["<x1"], lambda: sp.dma_start(XB[:, :], x[bass.ts(t, P), :]), dma=True)
            scores = SA[:, :, 0:2 * NKV].rearrange("p a (h j) -> p a h j", j=NKV)

            def before(name, g, back):
                return f"{name}_{g - back}" if g >= back else f"<{name}_{g - back + GROUPS}"

            def score_products(g):
                for i in range(2):
                    pe.matmul(SA[:, i, 0:2 * NKV], identb[:, :], MASK[:, :].unsqueeze(1).to_broadcast([P, 2, NKV]),
                              start=True, stop=False, skip_group_check=True)
                    for j in range(2):
                        h = g * GH + 2 * i + j
                        slot = h % HB * KD + h // HB
                        last = pe.matmul(SA[:, i, j * NKV:(j + 1) * NKV], QS[:, slot, :], KN[:, slot, :],
                                         start=False, stop=True, skip_group_check=True)
                return last

            def exp_transposes(e):
                for hh in range(GH):
                    pe.transpose(TA[:, hh * P:(hh + 1) * P], EXPS[:, e, hh, 0:P], ident)
                for hh in range(GH):
                    last = pe.matmul(MA[RPAD * hh:RPAD * (hh + 1), 3 * P:4 * P], EXPS[:, e, hh, P:NPAD], ident,
                                     start=True, stop=True)
                return last

            def value_products(g):
                o = MA[:, 0:P]
                pe.matmul(o, VR[:, g * P:(g + 1) * P], PR[g % 2][:, :], start=True, stop=False, skip_group_check=True)
                for hh in range(GH):
                    h = g * GH + hh
                    last = pe.matmul(o[32 * hh:32 * hh + 32, :], VN[:, h * VW:(h + 1) * VW], PT[g % 2][:, hh, :],
                                     start=False, stop=True, skip_group_check=True)
                return last

            def tail(g):
                e = g % 2
                yield do("pe", f"exps_ps_{g}", [f"exps_{g}", before("ot", g, 1)] + (["<x1", "<on"] if g == 0 else []),
                   lambda: exp_transposes(e))
                yield do("dve", f"probr_{g}", [f"exps_ps_{g}", "A.countt", before("values", g, 2)],
                   lambda: dve.tensor_tensor(PR[e][:, :], MA[:, 3 * P:4 * P], COUNTT[:, 1, :], ALU.mult))
                yield do("dve", f"probs_{g}", [],
                   lambda: dve.tensor_tensor(PT[e][:, :, :], TA[:, :].rearrange("p (h q) -> p h q", h=GH),
                                             COUNTT[:, 0, :].unsqueeze(1).to_broadcast([P, GH, P]), ALU.mult))
                yield do("pe", f"values_{g}", [f"probs_{g}"], lambda: value_products(g))
                yield do("act", f"ot_{g}", [f"values_{g}"] + (["<ot_ps"] if g == 0 else []),
                   lambda: act.activation(OT[:, g, :], MA[:, 0:P], ACT.Copy))

            def head(g):
                e = g % 2
                yield do("pe", f"scores_{g}", ["A.know", "A.vnow", "A.qslabs0", "A.qslabs1", "A.qslabs2", "A.mask", before("exps", g, 1)], lambda: score_products(g))
                yield do("dve", f"max_{g}", [f"scores_{g}", before("exps", g, 2)],
                   lambda: dve.tensor_reduce(MAXS[:, e, :].rearrange("p (a h) -> p a h", a=2), scores, AX.X, ALU.max,
                                             negate=True))
                for hh in range(GH):
                    yield do("act", f"exps_{g}" if hh == GH - 1 else f"exps{hh}_{g}", [f"max_{g}", before("exps_ps", g, 2)],
                       lambda: act.activation(EXPS[:, e, hh, 0:NKV], scores[:, hh // 2, hh % 2, :], ACT.Exp,
                                              bias=MAXS[:, e, hh:hh + 1]))
            yield from head(0)
            for g in range(1, GROUPS):
                yield from in_turn(head(g), tail(g - 1))
            yield from tail(GROUPS - 1)
            yield do("pe", "ot_ps", ["ot_3", "probs_3"], lambda: transposes(TA[:, :], flat(OT[:, :, :]), GROUPS))
            attn = TA[:, :].rearrange("p (h w) -> p h w", w=VW)
            yield do("dve", "rsum", ["ot_ps"], lambda: dve.reciprocal(RSUM[:, :].unsqueeze(2), attn[:, :, DA:DA + 1]))
            yield do("dve", "on", ["rsum", "<ont_ps"],
               lambda: dve.tensor_tensor(ON[:, :].rearrange("p (h d) -> p h d", d=DA), attn[:, :, 0:DA],
                                         RSUM[:, :].unsqueeze(2).to_broadcast([P, HA, DA]), ALU.mult))
            yield do("pe", "ont_ps", ["on"], lambda: transposes(TA[:, :], ON[:, :], KD))
            yield do("act", "ont", ["ont_ps", "<y_ps"], lambda: act.activation(flat(ONT[:, :, :]), TA[:, 0:D], ACT.Copy))

            def y_product():
                for k in range(KD):
                    last = pe.matmul(TA[:, D:2 * D], ONT[:, k, :], WOUT[:, k, :], start=k == 0, stop=k == KD - 1)
                return last

            yield do("pe", "y_ps", ["ont"], y_product)
            yield do("dve", "x1", ["y_ps", "load_xb", "<<C.x1b", "<<C.xm"],
               lambda: dve.tensor_tensor(X1[:, :], TA[:, D:2 * D], XB[:, :], ALU.add))

        def cols(p):
            return slice(p * P, (p + 1) * P)

        def by_pairs(bank, lhs, rhs, contraction=1):
            for p in range(NP):
                for k in range(contraction):
                    last = pe.matmul(bank[:, cols(p)], lhs(k, p), rhs(k), start=k == 0, stop=k == contraction - 1)
            return last

        def part_c(t, odd, first):
            do = begin_c(t, first)
            X1, X1B, XMT, HQ, HALFE = X1S[odd], X1BS[odd], XMTS[odd], HQS[odd], HALFES[odd]
            CUME, TRIE, ISEXPT, LS3, SG = CUMES[odd], TRIES[odd], ISEXPTS[odd], LS3S[odd], SGS[odd]
            V, VM, K2 = VS[odd], VMS[odd], K2S[odd]
            C0 = F[:, 0, :]
            yield do("dve", "stats", ["B.x1"], lambda: dve.bn_stats(STATS2[:, :], X1[:, :]))
            yield do("dve", "meanvar", ["stats"], lambda: dve.bn_aggr(MV2[:, :], STATS2[:, :]), apart=True)
            yield do("pool", "x1b", ["B.x1", "<<D.out"], lambda: pool.tensor_copy(X1B[:, :], X1[:, :]), apart=True)
            yield do("act", "lnvar", ["meanvar"], lambda: act.activation(RSTD2[:, 0:1], MV2[:, 1:2], ACT.Ln, bias=eps))
            yield do("act", "rstd", ["lnvar"], lambda: act.activation(RSTD2[:, 1:2], RSTD2[:, 0:1], ACT.Exp, scale=-0.5))
            yield do("dve", "xm", ["rstd", "<xmt_ps"],
               lambda: dve.tensor_scalar(XM[:, :], X1[:, :], MV2[:, 0:1], RSTD2[:, 1:2], ALU.subtract, ALU.mult))
            yield do("pe", "xmt_ps", ["xm", "<k2shift", ">>A.xt"], lambda: transposes(C0, XM[:, :], KD))
            yield do("act", "xmt", ["xmt_ps", "<<D.k1_ps"], lambda: act.activation(flat(XMT[:, :, :]), C0[:, 0:D], ACT.Copy))

            def hidden():
                for k in range(KD):
                    pe.matmul(C0[:, 0:NE], XMT[:, k, :], WE[:, k, :], start=k == 0, stop=k == KD - 1)
                for m in range(2):
                    for k in range(KD):
                        last = pe.matmul(C0[:, (2 + m) * P:(3 + m) * P], WA[:, k, m * P:(m + 1) * P], XMT[:, k, :],
                                         start=k == 0, stop=k == KD - 1)
                return last

            yield do("pe", "hidden_ps", ["xmt", ">>A.qt"], hidden)
            yield do("act", "hid2", ["hidden_ps", "<zg_ps", "<zpart2"],
               lambda: act.activation(HID2[:, :], C0[:, 3 * P:4 * P], ACT.Identity, bias=const("onerow")))
            yield do("act", "hid1", ["<k2_ps", "<hq"], lambda: act.activation(HID1[:, :], C0[:, 2 * P:3 * P], ACT.Copy))
            yield do("act", "logit", [], lambda: act.activation(LOGIT[:, :], C0[:, 0:NE], ACT.Copy))
            yield do("act", "zpart0", ["hid2", "<zstore0", "<zstore1"],
               lambda: act.activation(ZPARTS[:, 0, :], HID2[:, :], ACT.Copy))
            yield do("pool", "zrest", ["zpart0", "<zpart2"],
               lambda: pool.tensor_tensor(ZREST[:, :], HID2[:, :], ZPARTS[:, 0, :], ALU.subtract))
            yield do("act", "zpart1", ["zrest"], lambda: act.activation(ZPARTS[:, 1, :], ZREST[:, :], ACT.Copy))
            yield do("pool", "zpart2", ["zpart1", "<z1_ps", "<zslabs0", "<zslabs1", "<zslabs2"],
               lambda: pool.tensor_tensor(ZPARTS[:, 2, :], ZREST[:, :], ZPARTS[:, 1, :], ALU.subtract), apart=True)
            z_rows = z_dram.rearrange("(n r) (g t) -> r g n t", n=PARTS, g=2)
            for g in range(2):
                first_row = P // 2 + 32 * g
                yield do("sp", f"zstore{g}", ["zpart2"],
                   lambda: sp.dma_start(z_rows[:, g], ZPARTS[first_row:first_row + GR, :, :]), dma=True)
            for n in range(PARTS):
                slabs = slice(n * PARTS, min(n * PARTS + PARTS, len(Z_SLABS)))
                yield do("sp", f"zslabs{n}", ["zstore0", "zstore1"],
                   lambda: sp.dma_start(ZS[slabs.start * GR:slabs.stop * GR, :, :].rearrange("r g t -> r (g t)"),
                                        z_dram[0:(slabs.stop - slabs.start) * GR, :]), dma=True)
            yield do("dve", "rmax", ["logit"], lambda: dve.tensor_reduce(RT[:, 0:1], LOGIT[:, :], AX.X, ALU.max))
            yield do("dve", "rnmax", [], lambda: dve.tensor_reduce(RT[:, 1:2], LOGIT[:, :], AX.X, ALU.max, negate=True))
            yield do("dve", "rvals", ["rmax"],
               lambda: dve.scalar_tensor_tensor(VALS[:, :], LOGIT[:, :], RT[:, 0:1], prio, ALU.is_equal, ALU.mult))
            yield do("dve", "label", ["rvals"], lambda: dve.tensor_reduce(RT[:, 4:5], VALS[:, :], AX.X, ALU.max))
            yield do("act", "rexp", ["rnmax"], lambda: act.activation(ELOG[:, :], LOGIT[:, :], ACT.Exp, bias=RT[:, 1:2]))
            yield do("dve", "labb", ["label"], lambda: dve.tensor_copy(LABB[:, :], RT[:, 4:5]))
            yield do("dve", "isexp", [], lambda: dve.tensor_scalar(ISEXP[:, :], prio, RT[:, 4:5], None, ALU.is_equal))
            yield do("dve", "rsum", ["rexp"], lambda: dve.tensor_reduce(RT[:, 2:3], ELOG[:, :], AX.X, ALU.add))
            yield do("dve", "halfe", ["isexp", "<<D.sums_ps"],
               lambda: dve.tensor_tensor(
                   HALFE[:, :, :, :], const("half").unsqueeze(1).unsqueeze(3).to_broadcast([P, 2, 2, EH]),
                   ISEXP[:, :].rearrange("p (e c) -> p c e", c=2).unsqueeze(2).to_broadcast([P, 2, 2, EH]), ALU.mult))
            yield do("dve", "rweight", ["rsum"], lambda: dve.reciprocal(RT[:, 3:4], RT[:, 2:3]))
            yield do("pe", "zg_ps", ["logit"],
               lambda: by_pairs(C0, lambda k, p: WGB[0:64, cols(p)], lambda k: HID2[0:64, :]))
            yield do("act", "zabs2", ["zg_ps", "<ls2"], lambda: act.activation(ZABS[:, 2, :], C0, ACT.Abs))
            yield do("act", "zg", ["<<D.osg"], lambda: act.activation(SG[:, :], C0, ACT.Copy))
            yield do("dve", "zmin2", ["zg", "<<D.osg"],
               lambda: dve.tensor_scalar(LS3[:, 2, :], C0, 0.0, None, ALU.min))

            def v_product():
                for k in range(KD):
                    last = pe.matmul(C0, XMT[:, k, :], WV[:, k, :], start=k == 0, stop=k == KD - 1)
                return last

            yield do("pe", "v_ps", ["zmin2", "zg"], v_product)
            yield do("act", "zexp2", ["zabs2"], lambda: act.activation(ZABS[:, 2, :], ZABS[:, 2, :], ACT.Exp, scale=-1.0))
            yield do("act", "zln2", ["zexp2"], lambda: act.activation(ZABS[:, 2, :], ZABS[:, 2, :], ACT.Ln, bias=1.0))
            yield do("act", "v", ["v_ps", "<<D.kvd_ps"], lambda: act.activation(V[:, :], C0, ACT.Copy))
            yield do("pool", "ls2", ["zln2", "zmin2"],
               lambda: pool.tensor_tensor(LS3[:, 2, :], LS3[:, 2, :], ZABS[:, 2, :], ALU.subtract))
            slab_rows = slice(0, len(Z_SLABS) * GR)
            yield do("pe", "z0_ps", ["v", "zslabs0", "zslabs1", "zslabs2"],
               lambda: pe.matmul(C0, ZS[slab_rows, 0, :], ZW[slab_rows, 0, :], start=True, stop=True))
            yield do("act", "zabs0", ["z0_ps", "<ls"], lambda: act.activation(ZABS[:, 0, :], C0, ACT.Abs))
            yield do("dve", "zmin0", ["zabs0", "<<D.sums_ps"],
               lambda: dve.tensor_scalar(LS3[:, 0, :], C0, 0.0, None, ALU.min))
            yield do("pe", "z1_ps", ["zmin0", "zabs0"],
               lambda: pe.matmul(C0, ZS[slab_rows, 1, :], ZW[slab_rows, 1, :], start=True, stop=True))
            yield do("act", "zabs1", ["z1_ps"], lambda: act.activation(ZABS[:, 1, :], C0, ACT.Abs))
            yield do("dve", "zmin1", ["zabs1"], lambda: dve.tensor_scalar(LS3[:, 1, :], C0, 0.0, None, ALU.min))
            yield do("act", "zexp", ["zabs1"],
               lambda: act.activation(ZABS[:, 0:2, :], ZABS[:, 0:2, :], ACT.Exp, scale=-1.0))
            yield do("act", "zln", ["zexp"], lambda: act.activation(ZABS[:, 0:2, :], ZABS[:, 0:2, :], ACT.Ln, bias=1.0))

            def router_rows():
                pe.matmul(C0[:, 0:P], RT[:, 3:4].to_broadcast([P, P]), ident, start=True, stop=True)
                return pe.matmul(C0[:, P:2 * P], LABB[:, 0:1].to_broadcast([P, P]), identb[:, :], start=True, stop=True)

            yield do("pe", "rows_ps", ["zmin1", "zabs1", "labb", "rweight"], router_rows)
            yield do("pool", "ls", ["zln", "zmin1"],
               lambda: pool.tensor_tensor(LS3[:, 0:2, :], LS3[:, 0:2, :], ZABS[:, 0:2, :], ALU.subtract))
            yield do("dve", "hq", ["rows_ps", "<<D.q2_ps"],
               lambda: dve.tensor_tensor(HQ[0:64, :], HID1[0:64, :], C0[0:64, 0:P], ALU.mult))
            label_row = C0[:, P:2 * P]
            yield do("dve", "cume", ["<<D.g2_ps"],
               lambda: dve.scalar_tensor_tensor(CUME[:, :], label_row, RT[:, 4:5], cum, ALU.is_equal, ALU.mult))
            yield do("dve", "trie", ["<<D.at2"],
               lambda: dve.scalar_tensor_tensor(TRIE[:, :], label_row, RT[:, 4:5], tri, ALU.is_equal, ALU.mult))
            yield do("dve", "isexpt", ["<<D.qm"],
               lambda: dve.tensor_tensor(ISEXPT[:, :, :], label_row.unsqueeze(1).to_broadcast([P, EH, P]),
                                         const("prio_half").unsqueeze(2).to_broadcast([P, EH, P]), ALU.is_equal))
            for e in range(NE):
                yield do("act", "vm" if e == NE - 1 else f"vm{e}", ["v", "isexp", "<<D.kv_ps"],
                   lambda e=e: act.activation(VM[:, :, e % 2, e // 2, :], V[:, :].rearrange("p (h d) -> p h d", d=DK), ACT.Copy,
                                              scale=ISEXP[:, e:e + 1]))
            yield do("act", "sigm", ["ls2"], lambda: act.activation(LS3[:, 2, :], LS3[:, 2, :], ACT.Exp))
            yield do("pe", "k2_ps", ["isexpt", ">>A.countt"],
               lambda: pe.matmul(C0, HID1[64:128, :], WQKB[64:128, :], start=True, stop=True))
            yield do("pool", "sg", ["sigm"],
               lambda: pool.tensor_tensor(SG[:, :], SG[:, :], LS3[:, 2, :], ALU.mult))
            k2p = C0.rearrange("p (h d) -> p h d", d=DK)
            yield do("dve", "k2max", ["k2_ps"], lambda: dve.tensor_reduce(KS[:, 0, :], k2p, AX.X, ALU.max))
            yield do("dve", "k2shift", ["k2max", "<<D.k2t_ps"],
               lambda: dve.tensor_tensor(K2[:, :, :], k2p, KS[:, 0, :].unsqueeze(2).to_broadcast([P, H, DK]),
                                         ALU.subtract))
            yield do("act", "k2exp", ["k2shift"], lambda: act.activation(K2[:, :, :], K2[:, :, :], ACT.Exp))
            yield do("dve", "k2sum", ["k2exp"], lambda: dve.tensor_reduce(KS[:, 1, :], K2[:, :, :], AX.X, ALU.add))
            yield do("dve", "k2rec", ["k2sum"], lambda: dve.reciprocal(KS[:, 2, :], KS[:, 1, :]))
            yield do("dve", "k2w", ["k2rec"], lambda: dve.tensor_scalar(KS[:, 3, :], KS[:, 2, :], RT[:, 3:4], None, ALU.mult))
            yield do("dve", "k2", ["k2w"],
               lambda: dve.tensor_tensor(K2[:, :, :], K2[:, :, :], KS[:, 3, :].unsqueeze(2).to_broadcast([P, H, DK]),
                                         ALU.mult))

        def part_d(t, odd, first):
            do = begin_d(t, first)
            X1B, XMT, HQ, HALFE = X1BS[odd], XMTS[odd], HQS[odd], HALFES[odd]
            CUME, TRIE, ISEXPT, LS3, SG = CUMES[odd], TRIES[odd], ISEXPTS[odd], LS3S[odd], SGS[odd]
            V, VM, K2 = VS[odd], VMS[odd], K2S[odd]
            D0, D1, D2 = (F[:, n, :] for n in (1, 2, 3))
            D12 = F[:, 2:4, :].rearrange("p a (b c) -> p a b c", c=P)
            yield do("pe", "g1_ps", ["C.ls", "<osg"], lambda: by_pairs(D0, lambda k, p: LS3[:, 0, cols(p)], lambda k: cum))
            yield do("pe", "q1_ps", ["C.xmt", "<out"],
               lambda: by_pairs(D1, lambda k, p: WQ[:, k, cols(p)], lambda k: XMT[:, k, :], KD))
            yield do("act", "ep1", ["g1_ps"], lambda: act.activation(EP[:, :], D0, ACT.Exp))
            yield do("act", "en1", [], lambda: act.activation(EN1[:, :], D0, ACT.Exp, scale=-1.0))
            yield do("pe", "k1_ps", ["<rmsln"],
               lambda: by_pairs(D2, lambda k, p: WK[:, k, cols(p)], lambda k: XMT[:, k, :], KD))
            yield do("dve", "q1", ["q1_ps", "en1", "<o_ps"],
               lambda: dve.scalar_tensor_tensor(flat(Q1[:, :, :]), D1, DK ** -0.5, EP[:, :], ALU.mult, ALU.mult))
            yield do("dve", "k1", ["k1_ps"], lambda: dve.tensor_tensor(flat(KG1T[:, :, :]), D2, EN1[:, :], ALU.mult))
            yield do("pe", "g2_ps", ["C.cume", "en1"],
               lambda: by_pairs(D0, lambda k, p: LS3[:, 1, cols(p)], lambda k: CUME[:, :]))
            yield do("act", "en2", ["g2_ps"], lambda: act.activation(EN2[:, :], D0, ACT.Exp, scale=-1.0))
            yield do("act", "ep2", ["q1"], lambda: act.activation(EP[:, :], D0, ACT.Exp))
            yield do("pe", "q2_ps", ["q1", "C.hq"],
               lambda: by_pairs(D1, lambda k, p: WQKB[0:64, cols(p)], lambda k: HQ[0:64, :]))
            yield do("pe", "k2t_ps", ["C.k2", "ep2"], lambda: transposes(D0, K2[:, :, :].rearrange("p h d -> p (h d)"), NP))
            yield do("dve", "q2", ["q2_ps", "ep2", "<qm"],
               lambda: dve.scalar_tensor_tensor(flat(QG2[:, :, :]), D1, DK ** -0.5, EP[:, :], ALU.mult, ALU.mult))
            for par in range(2):
                for ep in range(2):
                    yield do("sp", f"qd{par}{ep}", ["q2"],
                       lambda: sp.dma_start(QD[DK * ep:DK * ep + DK, par, :, :], QG2[DK * par:DK * par + DK, :, :]), dma=True)
            for e in range(EH):
                yield do("pool", "qm" if e == EH - 1 else f"qm{e}", ["qd00", "qd01", "qd10", "qd11", "<o_ps"],
                   lambda: pool.tensor_tensor(QM[:, e, :, :, :].rearrange("p a b t -> p (a b) t"),
                                              QD[:, :, :, :].rearrange("p a b t -> p (a b) t"),
                                              ISEXPT[:, e, :].unsqueeze(1).to_broadcast([P, H, P]), ALU.mult))
            yield do("dve", "kg2", ["k2t_ps", "en2"],
               lambda: dve.tensor_tensor(flat(KG2T[:, :, :]), D0, EN2[:, :], ALU.mult))

            def inner(kt, q):
                for p in range(NP):
                    for par in range(2):
                        r = slice(64 * par, 64 * par + 64)
                        last = pe.matmul((D1, D2)[par][:, cols(p)], kt[r, p, :], q[r, p, :], start=True, stop=True)
                return last

            yield do("pe", "a1_ps", ["q2", "k1"], lambda: inner(KG1T, Q1))
            yield do("pe", "k1t_ps", ["kg2"], lambda: transposes(D0, flat(KG1T[:, :, :]), NP))
            yield do("dve", "at1", ["a1_ps", "<o_inner"],
               lambda: dve.tensor_tensor(AT1[:, :, :, :].rearrange("p a b c -> p (a b) c"),
                                         D12.rearrange("p a b c -> p (a b) c"),
                                         tri.unsqueeze(1).to_broadcast([P, 2 * NP, P]), ALU.mult))
            yield do("act", "kg1", ["k1t_ps", "<kvd_ps"], lambda: act.activation(KG1[:, :], D0, ACT.Copy))
            yield do("pe", "k2gt_ps", ["kg1"], lambda: transposes(D0, flat(KG2T[:, :, :]), NP))
            yield do("pe", "a2_ps", ["at1"], lambda: inner(KG2T, QG2[:, :, :]))
            yield do("act", "kg2e", ["k2gt_ps", "<kv_ps"], lambda: act.activation(KG2[:, :], D0, ACT.Copy))
            yield do("dve", "at2", ["a2_ps", "<at"],
               lambda: dve.tensor_tensor(AT2[:, :, :, :].rearrange("p a b c -> p (a b) c"),
                                         D12.rearrange("p a b c -> p (a b) c"),
                                         TRIE[:, :].unsqueeze(1).to_broadcast([P, 2 * NP, P]), ALU.mult))

            yield do("pool", "at", ["at2"], lambda: pool.tensor_tensor(AT1[:, :, :, :], AT1[:, :, :, :], AT2[:, :, :, :], ALU.add))

            def half_sums(p):
                o = D0[:, 0:2 * (NS + NP)].rearrange("p (a n) -> p a n", a=2)
                pe.matmul(o[:, :, NS + p], LS3[:, 0, cols(p)], const("half"), start=True, stop=True)
                for h in (2 * p, 2 * p + 1):
                    for ep in range(2):
                        last = pe.matmul(o[DK * ep:DK * ep + DK, :, h * EH:(h + 1) * EH], LS3[:, 1, h * DK:(h + 1) * DK],
                                         HALFE[:, ep, :, :], start=True, stop=True)
                return last

            for p in range(NP):
                yield do("pe", "sums_ps" if p == NP - 1 else f"sums{p}", ["kg2e"], lambda: half_sums(p))
            yield do("act", "eg", ["sums_ps", "<elast"],
               lambda: act.activation(EG[:, :, :].rearrange("p a n -> p (a n)"), D0[:, 0:2 * (NS + NP)], ACT.Exp))
            yield do("dve", "dec", ["eg", "<decayd"],
               lambda: dve.scalar_tensor_tensor(DEC[:, :], ELAST[:, :],
                                                CONST[:, bass.ds(_C["keep"][0] + t, 1)],
                                                EG[:, 0, :], ALU.mult, ALU.mult))
            yield do("dve", "elast", ["dec"], lambda: dve.tensor_copy(ELAST[:, :], EG[:, 1, :]))
            states = STATE[:, :, :, :].rearrange("p h e d -> p (h e) d")
            yield do("pool", "decay", ["dec", "<state0"],
               lambda: pool.tensor_tensor(states, states, DEC[:, 0:NS].unsqueeze(2).to_broadcast([P, NS, DK]), ALU.mult))
            yield do("pool", "decayd", ["<stated"],
               lambda: pool.tensor_tensor(STATED[:, :, :], STATED[:, :, :],
                                          DEC[:, NS:NS + NP].unsqueeze(2).to_broadcast([P, NP, DK]), ALU.mult))

            def kv_products():
                for h in range(H):
                    for ep in range(2):
                        o = F[DK * ep:DK * ep + DK, 2 + h // 4, (h % 4) * EH * DK:(h % 4 + 1) * EH * DK]
                        last = pe.matmul(o, KG2[:, h * DK:(h + 1) * DK], VM[:, h, ep, :, :].rearrange("p e d -> p (e d)"),
                                         start=True, stop=True)
                return last

            def dense_kv_products():
                for p in range(NP):
                    for par in range(2):
                        h = 2 * p + par
                        c = slice(h * DK, (h + 1) * DK)
                        last = pe.matmul(D1[64 * par:64 * par + 64, p * DK:(p + 1) * DK], KG1[:, c], V[:, c],
                                         start=True, stop=True)
                return last

            def inner_outputs():
                for p in range(NP):
                    for par in range(2):
                        h = 2 * p + par
                        last = pe.matmul(D0[64 * par:64 * par + 64, cols(p)], V[:, h * DK:(h + 1) * DK],
                                         AT1[:, par, p, :], start=p == 0, stop=False, skip_group_check=True)
                return last

            def state_outputs():
                for p in range(NP):
                    for e in range(EH):
                        for par in range(2):
                            pe.matmul(D0[DK * par:DK * par + DK, cols(p)], STATE[:, 2 * p + par, e, :], QM[:, e, par, p, :],
                                      start=False, stop=False, skip_group_check=True)
                    for par in range(2):
                        r = slice(DK * par, DK * par + DK)
                        last = pe.matmul(D0[r, cols(p)], STATED[r, p, :], Q1[r, p, :], start=False, stop=True,
                                         skip_group_check=True)
                return last

            yield do("pe", "kv_ps", ["at2", "C.vm"], kv_products)
            yield do("pe", "o_inner", ["at", "eg"], inner_outputs)
            yield do("pe", "o_ps", ["decayd", "qm"], state_outputs, apart=True)
            for n, name in ((1, "state1"), (0, "state0")):
                heads = STATE[:, n * H // 2:(n + 1) * H // 2, :, :].rearrange("p h e d -> p (h e d)")
                yield do("dve", name, ["o_ps"], lambda: dve.tensor_tensor(heads, heads, F[:, 2 + n, :], ALU.add))
            yield do("act", "sq", ["o_ps", "<rmsog"], lambda: act.activation(RMS[:, :], D0, ACT.Square))
            yield do("dve", "osg", ["sq", "C.sg", "<y_ps"],
               lambda: dve.tensor_tensor(flat(OG[:, :, :]), D0, SG[:, :], ALU.mult))
            yield do("pe", "ms_ps", ["sq", "state1"], lambda: pe.matmul(D2, const("pairs"), RMS[:, :], start=True, stop=True))
            yield do("pe", "kvd_ps", ["state0"], dense_kv_products)
            yield do("act", "rmsln", ["ms_ps"], lambda: act.activation(RMS[:, :], D2, ACT.Ln, bias=eps))
            yield do("act", "rms", ["rmsln"], lambda: act.activation(RMS[:, :], RMS[:, :], ACT.Exp, scale=-0.5))
            yield do("dve", "stated", ["kvd_ps"],
               lambda: dve.tensor_tensor(flat(STATED[:, :, :]), flat(STATED[:, :, :]), D1[:, 0:NP * DK], ALU.add))
            yield do("dve", "rmsog", ["rms", "osg"],
               lambda: dve.tensor_tensor(flat(OG[:, :, :]), flat(OG[:, :, :]), RMS[:, :], ALU.mult))

            def out_product():
                for p in range(NP):
                    last = pe.matmul(D1[:, D:2 * D], OG[:, p, :], WO[:, p, :], start=p == 0, stop=p == NP - 1)
                return last

            yield do("pe", "y_ps", ["rmsog"], out_product)
            yield do("dve", "out", ["y_ps", "C.x1b", "<store"],
               lambda: dve.tensor_tensor(OUT[:, :], D1[:, D:2 * D], X1B[:, :], ALU.add))
            yield do("sp", "store", ["out"], lambda: sp.dma_start(out[bass.ts(t, P), :], OUT[:, :]), dma=True)

        parts = (part_a, part_b, part_c, part_d)
        lag = len(parts) - 1

        def iteration(i, odd, first):
            running = {}
            for n, part in enumerate(parts):
                if first - n >= 0 and not (isinstance(i, int) and i - n >= TILES):
                    running["ABCD"[n]] = part(i - n, (odd + n) % 2, first - n)
            for name in order:
                if name in running:
                    next(running[name], None)
            assert all(next(g, "end") == "end" for g in running.values())

        length = {name: sum(1 for _ in part(0, 0, 0)) for name, part in zip("ABCD", parts)}
        order = "".join(run[0] * int(run[1:]) for run in ORDER.split())
        assert all(order.count(n) == length[n] for n in length), length
        steps.dry = False
        start = lag + 1
        for i in range(start):
            iteration(i, i % 2, i)
        with nc.Fori(start // 2, TILES // 2) as pair:
            for odd in range(2):
                iteration(pair * 2 + odd, odd, start + odd)
        for i in range(TILES, TILES + lag):
            iteration(i, i % 2, i)
        steps.wait("D", "sp", "store")


def in_turn(*parts):
    live = list(parts)
    while live:
        for g in list(live):
            if next(g, "end") == "end":
                live.remove(g)
            else:
                yield


def kernel(**inputs):
    import concourse.bacc as bacc
    from concourse.bass_utils import run_bass_kernel_spmd

    def a(name):
        return np.asarray(inputs[name])

    def blocks(w):
        return np.ascontiguousarray(w.reshape(-1, P, w.shape[1]).transpose(1, 0, 2))

    def heads_inside(w):
        return w.reshape(-1, KD, HB, DA).transpose(0, 1, 3, 2).reshape(-1, D)

    f = "L0_ffn_"
    pad = np.zeros((D, 16), np.float32)
    gap = np.zeros((15, HD), np.float32)
    arrays = {
        "x": a("x").reshape(B * L, D),
        "idx": a("itok_BxSx64_0_2047").reshape(B * L, PICKS),
        "ctxT": blocks(a("ctx_1024").reshape(B * NKV, D).T),
        "consts": constants(),
        "w_q": blocks(heads_inside(a("L0_xattn_W_q").T)),
        "w_down": blocks(a("L0_xattn_W_kv_down").T),
        "w_up": np.concatenate([heads_inside(a("L0_xattn_W_kv_up").T[:, :D]), a("L0_xattn_W_kv_up").T[:, D:]], 1),
        "w_out": blocks(a("L0_xattn_W_out").T),
        "wa": blocks(np.concatenate([a(f + "Wqa"), a(f + "Wka"), a(f + "Wga"), a(f + "Wg1a"), pad, a(f + "Wg2a"), pad], 1)),
        "we": blocks(a(f + "We")),
        "wq": blocks(a(f + "Wq")),
        "wk": blocks(a(f + "Wk")),
        "wv": blocks(a(f + "Wv")),
        "wqk_b": np.concatenate([a(f + "Wqb"), a(f + "Wkb")]),
        "wg_b": np.concatenate([a(f + "Wgb"), a(f + "Wg1b"), a(f + "bg1")[None], gap, a(f + "Wg2b"), a(f + "bg2")[None], gap]),
        "wo": blocks(a(f + "Wo")),
        "norm_w": np.concatenate([a(f + "norm_w"), a(f + "norm_w")])[:, None],
    }
    nc = bacc.Bacc("TRN2", target_bir_lowering=False, num_devices=1)
    args, fed = [], {}
    for name, v in arrays.items():
        v = np.ascontiguousarray(v)
        fed[name + "_dram"] = v
        args.append(nc.dram_tensor(name + "_dram", v.shape, mybir.dt.from_np(v.dtype), kind="ExternalInput").ap())
    out = nc.dram_tensor("out_dram", (B * L, D), mybir.dt.float32, kind="ExternalOutput").ap()
    program(nc, *args, out)
    r = run_bass_kernel_spmd(nc, [fed], core_ids=[0])
    return r.results[0]["out_dram"].reshape(B, L, D)
```
